# Optimizing a Trainium2 kernel written in Bass

```python
import numpy as np
import jax
import jax.numpy as jnp

def _softmax(x, axis=-1):
    return jax.nn.softmax(x, axis=axis)

def _gelu(x):
    return jax.nn.gelu(x, approximate=True)

def _silu(x):
    return jax.nn.silu(x)

def _sigmoid(x):
    return jax.nn.sigmoid(x)

def _layernorm(x, axis=-1, eps=1e-05):
    m = jnp.mean(x, axis=axis, keepdims=True)
    v = jnp.var(x, axis=axis, keepdims=True)
    return (x - m) / jnp.sqrt(v + eps)

def _scatter_add(tgt, idx, src, axis=0):
    return tgt.at[idx].add(src)

def _segment_sum(src, seg, n):
    return jax.ops.segment_sum(src, seg, n)
kernel_name = 'mk_xattn_ffn_d1_seqx_r8_9e6e47'

def setup_inputs(seed: int=0):
    np.random.seed(seed)
    _w = jnp.asarray

    def _rec_inputs():
        import jax
        import jax.numpy as jnp
        _rk = jax.random.key(seed)
        x = -0.0002928 + 1 * jax.random.normal(jax.random.fold_in(_rk, 1), (16, 128, 256), jnp.float32)
        _lenS = 128 - jax.random.randint(jax.random.fold_in(_rk, 7), (16,), 0, max(1, 128 // 4) + 1, jnp.int32)
        _lenS2 = 128 - jax.random.randint(jax.random.fold_in(_rk, 8), (16,), 0, max(1, 128 // 4) + 1, jnp.int32)
        fside_S2_0 = -0.00337071 + 1.01897 * jax.random.normal(jax.random.fold_in(_rk, 11), (128,), jnp.float32)
        _ctx_2048P = jax.random.normal(jax.random.fold_in(_rk, 12), (16, 16, 256), jnp.float32)
        _ctx_2048c = jax.random.dirichlet(jax.random.fold_in(_rk, 512), 0.3 * jnp.ones((16,), jnp.float32), (16, 128))
        _ctx_2048t = jnp.einsum('bsk,bkd->bsd', _ctx_2048c, _ctx_2048P)
        _ctx_2048t = _ctx_2048t * jax.lax.rsqrt(jnp.mean(jnp.square(_ctx_2048t)) + 1e-12) * 0.953939
        ctx_2048 = 0.000675642 + 1.00031 * (_ctx_2048t + 0.3 * jax.random.normal(jax.random.fold_in(_rk, 612), (16, 128, 256), jnp.float32))
        return (x, fside_S2_0, ctx_2048)
    x, fside_S2_0, ctx_2048 = _rec_inputs()

    def _L0_xattn_setup():
        import jax, jax.numpy as jnp
        import numpy as np
        key = jax.random.key(seed)
        ks = jax.random.split(key, 5)
        B, D, L, NH = (2, 128, 256, 8)
        H = D // NH
        return {'v': jax.random.normal(ks[0], (B, D, L), jnp.float32), 'k': jax.random.normal(ks[1], (H, L), jnp.float32) * 0.1, 'bias': jax.random.normal(ks[2], (D,), jnp.float32), 'x1': jax.random.normal(ks[3], (B, D, L), jnp.float32), 'x2': jax.random.normal(ks[4], (B, D, L), jnp.float32), 'num_heads': NH}
    _L0_xattn_all = _L0_xattn_setup()
    _L0_xattn_in = {k: v for k, v in _L0_xattn_all.items() if k in ('k',)}
    del _L0_xattn_all

    def _L0_ffn_setup():
        import jax, jax.numpy as jnp
        import numpy as np
        DIM = 256
        INTER = 176
        E = 16
        TOPK = 4
        G = 4
        TOPK_G = 2
        N_SHARED = 2
        SHARED_INTER = N_SHARED * INTER
        ROUTE_SCALE = 1.0

        def _moe_forward(x, Wg, W1, W3, W2, Ws1, Ws3, Ws2):
            B, S, D = x.shape
            xt = x.reshape(-1, D)
            T = xt.shape[0]
            scores = jax.nn.softmax(xt @ Wg.T, axis=-1)
            sg = scores.reshape(T, G, E // G)
            group_scores = sg.max(axis=-1)
            gidx = jax.lax.top_k(group_scores, TOPK_G)[1]
            gmask = jax.nn.one_hot(gidx, G, dtype=jnp.float32).sum(axis=1) > 0
            masked = jnp.where(gmask[:, :, None], sg, -jnp.inf).reshape(T, E)
            topi = jax.lax.top_k(masked, TOPK)[1]
            weights = jnp.take_along_axis(scores, topi, axis=1) * ROUTE_SCALE
            combine = jnp.zeros((T, E), xt.dtype).at[jnp.arange(T)[:, None], topi].add(weights)
            h = jax.nn.silu(jnp.einsum('td,eid->eti', xt, W1)) * jnp.einsum('td,eid->eti', xt, W3)
            expert_out = jnp.einsum('eti,edi->etd', h, W2)
            y = jnp.einsum('etd,te->td', expert_out, combine)
            z = jax.nn.silu(xt @ Ws1.T) * (xt @ Ws3.T) @ Ws2.T
            return (y + z).reshape(B, S, D)
        key = jax.random.key(seed)
        ks = jax.random.split(key, 8)
        s = 0.02
        x = jax.random.normal(ks[0], (1, 256, DIM), dtype=jnp.float32)
        Wg = jax.random.normal(ks[1], (E, DIM), dtype=jnp.float32) * s
        W1 = jax.random.normal(ks[2], (E, INTER, DIM), dtype=jnp.float32) * s
        W3 = jax.random.normal(ks[3], (E, INTER, DIM), dtype=jnp.float32) * s
        W2 = jax.random.normal(ks[4], (E, DIM, INTER), dtype=jnp.float32) * s
        Ws1 = jax.random.normal(ks[5], (SHARED_INTER, DIM), dtype=jnp.float32) * s
        Ws3 = jax.random.normal(ks[6], (SHARED_INTER, DIM), dtype=jnp.float32) * s
        Ws2 = jax.random.normal(ks[7], (DIM, SHARED_INTER), dtype=jnp.float32) * s
        return {'x': x, 'Wg': Wg, 'W1': W1, 'W3': W3, 'W2': W2, 'Ws1': Ws1, 'Ws3': Ws3, 'Ws2': Ws2}
    _L0_ffn_all = _L0_ffn_setup()
    _L0_ffn_in = {k: v for k, v in _L0_ffn_all.items() if k in ('Wg', 'W1', 'W3', 'W2', 'Ws1', 'Ws3', 'Ws2')}
    del _L0_ffn_all
    return {'x': x, 'fside_S2_0': fside_S2_0, 'ctx_2048': ctx_2048, 'L0_xattn_k': _L0_xattn_in['k'], 'L0_ffn_Wg': _L0_ffn_in['Wg'], 'L0_ffn_W1': _L0_ffn_in['W1'], 'L0_ffn_W3': _L0_ffn_in['W3'], 'L0_ffn_W2': _L0_ffn_in['W2'], 'L0_ffn_Ws1': _L0_ffn_in['Ws1'], 'L0_ffn_Ws3': _L0_ffn_in['Ws3'], 'L0_ffn_Ws2': _L0_ffn_in['Ws2']}

def reference(x, fside_S2_0, ctx_2048, L0_xattn_k, L0_ffn_Wg, L0_ffn_W1, L0_ffn_W3, L0_ffn_W2, L0_ffn_Ws1, L0_ffn_Ws3, L0_ffn_Ws2):
    import jax
    import jax.numpy as jnp

    def _L0_xattn_ref(v, k, bias, x1, x2, num_heads):
        import jax, jax.numpy as jnp
        import numpy as np
        B, D, L = v.shape
        H = D // num_heads
        fft_size = 2 * L
        vr = v.reshape(B, H, num_heads, L)
        x1r = x1.reshape(B, H, num_heads, L)
        x2r = x2.reshape(B, H, num_heads, L)
        kv = vr[:, :, :, None, :] * x2r[:, :, None, :, :]
        k_f = jnp.fft.rfft(k.astype(jnp.float32), n=fft_size)
        y = jnp.fft.irfft(jnp.fft.rfft(kv, n=fft_size) * k_f[None, :, None, None, :], n=fft_size)[..., :L]
        skip = bias.astype(jnp.float32).reshape(H, num_heads)[None, :, :, None, None]
        y = y + kv * skip
        out = jnp.einsum('bhijl,bhil->bhjl', y, x1r)
        return out.reshape(B, D, L)

    def _L0_ffn_ref(x, Wg, W1, W3, W2, Ws1, Ws3, Ws2):
        import jax, jax.numpy as jnp
        import numpy as np
        DIM = 256
        INTER = 176
        E = 16
        TOPK = 4
        G = 4
        TOPK_G = 2
        N_SHARED = 2
        SHARED_INTER = N_SHARED * INTER
        ROUTE_SCALE = 1.0

        def _moe_forward(x, Wg, W1, W3, W2, Ws1, Ws3, Ws2):
            B, S, D = x.shape
            xt = x.reshape(-1, D)
            T = xt.shape[0]
            scores = jax.nn.softmax(xt @ Wg.T, axis=-1)
            sg = scores.reshape(T, G, E // G)
            group_scores = sg.max(axis=-1)
            gidx = jax.lax.top_k(group_scores, TOPK_G)[1]
            gmask = jax.nn.one_hot(gidx, G, dtype=jnp.float32).sum(axis=1) > 0
            masked = jnp.where(gmask[:, :, None], sg, -jnp.inf).reshape(T, E)
            topi = jax.lax.top_k(masked, TOPK)[1]
            weights = jnp.take_along_axis(scores, topi, axis=1) * ROUTE_SCALE
            combine = jnp.zeros((T, E), xt.dtype).at[jnp.arange(T)[:, None], topi].add(weights)
            h = jax.nn.silu(jnp.einsum('td,eid->eti', xt, W1)) * jnp.einsum('td,eid->eti', xt, W3)
            expert_out = jnp.einsum('eti,edi->etd', h, W2)
            y = jnp.einsum('etd,te->td', expert_out, combine)
            z = jax.nn.silu(xt @ Ws1.T) * (xt @ Ws3.T) @ Ws2.T
            return (y + z).reshape(B, S, D)
        return _moe_forward(x, Wg, W1, W3, W2, Ws1, Ws3, Ws2)
    x = x + _L0_xattn_ref(_layernorm(x, axis=-1), L0_xattn_k, fside_S2_0, ctx_2048, ctx_2048, 8)
    x = x + _L0_ffn_ref(_layernorm(x, axis=-1), L0_ffn_Wg, L0_ffn_W1, L0_ffn_W3, L0_ffn_W2, L0_ffn_Ws1, L0_ffn_Ws3, L0_ffn_Ws2)
    return x

_drawn_inputs = setup_inputs


def setup_inputs(seed=0):
    import zlib

    import numpy as np

    out = dict(_drawn_inputs(seed))
    spreads = {}
    factors = {'L0_ffn_Wg': 8.0,
     'L0_ffn_W1': 8.0,
     'L0_ffn_W3': 8.0,
     'L0_ffn_W2': 8.0,
     'L0_ffn_Ws1': 8.0,
     'L0_ffn_Ws3': 8.0,
     'L0_ffn_Ws2': 8.0}
    for name, (base, spread) in spreads.items():
        noise = np.random.default_rng([zlib.crc32(name.encode()), seed]).standard_normal(out[name].shape)
        drawn = base * np.exp(spread * noise) if base else spread * noise
        out[name] = jnp.asarray(drawn.astype(out[name].dtype))
    for name, factor in factors.items():
        out[name] = (out[name] * factor).astype(out[name].dtype)
    return out
```

```python
from contextlib import ExitStack

import numpy as np

import concourse.bass as bass
from concourse import mybir

ALU = mybir.AluOpType
ACT = mybir.ActivationFunctionType
AX_X = mybir.AxisListType.X
F32 = mybir.dt.float32
BF16 = mybir.dt.bfloat16
I32 = mybir.dt.int32
U32 = mybir.dt.uint32

P = 128
B, D, L = 16, 128, 256
H, C = 16, 8
HH = H // 2
UNITS = B * D // P
LB = L // P
KV = HH * P
EPS = 1e-5

E, TOPK, G = 16, 4, 4
GE = E // G
TOP_G = 2
INTER = 176
HI = INTER // 2
NSH = 2
TOK = B * D
REGION = TOK + P
TILES = TOK * TOPK // P + E
ROW = L + 2 * E
SHARED = NSH * UNITS
STEPS = SHARED + TILES

HEADS = (0, 4, 1, 5)


def build(nc, x_d, ctx_d, ctxt_d, ctxr_d, k_d, bias_d, wg_d, w13_d, w2_d, out_d):
    kpad_d = nc.dram_tensor("kpad_scratch", (H, 3 * P), F32, kind="Internal").ap()
    rows_d = nc.dram_tensor("rows_scratch", ((E + 1) * REGION, ROW), F32, kind="Internal").ap()
    y_d = nc.dram_tensor("y_scratch", (TOPK * TOK + 2 * E * P, L), F32, kind="Internal").ap()

    with ExitStack() as ctx:
        def sb(name, shape, dt=F32):
            return ctx.enter_context(nc.sbuf_tensor(name, shape, dt))

        def sem(name):
            return ctx.enter_context(nc.semaphore(name))

        bank = [ctx.enter_context(nc.psum_tensor(f"bank{i}", [P, 512], F32)) for i in range(8)]

        w13 = sb("w13", [P, E + NSH, LB, 2 * INTER])
        w2 = sb("w2", [HI, E + NSH, 2, L])
        wg = sb("wg", [P, LB, E])
        toep = sb("toep", [P, H, L])
        ctx_rep = sb("ctx_rep", [P, 2, HH, L])
        kv = sb("kv", [P, 2, LB, KV])
        prod = sb("prod", [P, 4, 2, L])
        ctx_n = sb("ctx_n", [P, 2, L])
        ctx_tr = sb("ctx_tr", [P, 2, LB, P])
        v = sb("v", [P, 2, L])
        vc = sb("vc", [P, 2, L])
        v_tr = sb("v_tr", [P, 2, LB, P])
        xn = sb("xn", [P, 2, L])
        xn_tr = sb("xn_tr", [P, 2, LB, P])
        resid = sb("resid", [P, UNITS, L])
        rows = sb("rows", [P, UNITS, ROW])
        xn_tr_all = sb("xn_tr_all", [P, UNITS, LB, P])
        st1 = sb("st1", [P, 2, 16])
        st2 = sb("st2", [P, 2, 16])
        ident = sb("ident", [P, P])
        sum_i = sb("sum_i", [P, 2, 32])
        blocks = sb("blocks", [P, P])
        skip_w = sb("skip_w", [P, 2, P])
        bias_c = sb("bias_c", [P, 2])
        neg_half = sb("neg_half", [P, 1])
        before = sb("before", [P, P], BF16)
        ones = sb("ones", [P, P], BF16)
        low = sb("low", [P, G, G])
        io_e = sb("io_e", [P, E])
        io_tok = sb("io_tok", [P, UNITS, E])
        io_reg = sb("io_reg", [P, E])
        io_j = sb("io_j", [1, E])
        io_t = sb("io_t", [1, TILES])
        pad_row = sb("pad_row", [P, 2, ROW])
        top8 = sb("top8", [P, UNITS, 8])
        top_i = sb("top_i", [P, UNITS, 8], U32)
        sel_bf = sb("sel_bf", [P, UNITS, E], BF16)
        slot_i = sb("slot_i", [P, UNITS, TOPK], I32)
        tile_e = sb("tile_e", [1, TILES], I32)
        tile_row = sb("tile_row", [1, TILES], I32)
        pad_at = sb("pad_at", [1, E], I32)

        skip = vc
        kpad = prod[0:H, :, :, :].rearrange("p g h l -> p (g h l)")[:, 0:3 * P]
        kv_flat = kv[:].rearrange("p q b n -> p (q b n)")
        onehot = kv_flat[:, 0:1024].rearrange("p (t k e) -> p t k e", t=UNITS, k=TOPK)
        wide = kv_flat[:, 1024:2048]
        rt = ctx_rep[:].rearrange("p q h l -> p (q h) l")
        wide_m = kv_flat[0:1, 2048:2048 + TILES * E].rearrange("p (t e) -> p t e", e=E)
        meta = kv_flat[0:1, 2048 + TILES * E:2048 + TILES * (E + 6)].rearrange("p (i t) -> p i t", i=6)
        tf = toep[:].rearrange("p h l -> p (h l)")
        cut = [0]

        def carve(n):
            cut[0] += n
            return tf[:, cut[0] - n:cut[0]]

        xg = [carve(ROW) for _ in range(2)]
        x_tr = [carve(L).rearrange("p (b n) -> p b n", b=LB) for _ in range(2)]
        act1 = [carve(INTER) for _ in range(2)]
        hid = [carve(INTER) for _ in range(2)]
        hid_tr = [carve(2 * P)[0:HI, :].rearrange("p (b n) -> p b n", b=2) for _ in range(2)]
        y_sb = [carve(L) for _ in range(2)]
        gate_c = [carve(2) for _ in range(2)]
        dest_i = [sb(f"dest_i{i}", [P, 1], I32) for i in range(2)]
        fin = [ctx_rep[:, i, 0:TOPK, :] for i in range(2)]
        fin_a = [kv_flat[:, 2048 * i:2048 * i + L] for i in range(2)]
        fin_b = [kv_flat[:, 2048 * i + L:2048 * i + 2 * L] for i in range(2)]
        fin_o = [kv_flat[:, 2048 * i + 2 * L:2048 * i + 3 * L] for i in range(2)]

        y_ps = [bank[i][:, :].rearrange("p (h l) -> p h l", h=2) for i in range(4)]
        o_ps = bank[4][:, 0:L]
        g_ps = bank[5][:, 0:L]
        tr_ps = bank[6][:, 0:L].rearrange("p (b n) -> p b n", b=LB)
        logit_ps = bank[7][:, 0:UNITS * E]
        rank_ps = bank[6][:, 0:UNITS * E].rearrange("p (t e) -> p t e", e=E)
        count_ps = bank[6][:, 256:256 + UNITS * E].rearrange("p (t e) -> p t e", e=E)
        up_ps = [bank[i][:, 0:2 * INTER] for i in (0, 1)]
        ht_ps = [bank[i][0:HI, 0:2 * P].rearrange("p (b n) -> p b n", b=2) for i in (2, 3)]
        dn_ps = [bank[i][:, 0:L] for i in (4, 5)]
        xt_ps = [bank[i][:, 0:L].rearrange("p (b n) -> p b n", b=LB) for i in (6, 7)]

        wait_taken = sem("wait_taken")
        k_in, k_zero, k_out, toep_in = sem("k_in"), sem("k_zero"), sem("k_out"), sem("toep_in")
        bias_in, wg_in, wsh_in, w_in = sem("bias_in"), sem("wg_in"), sem("wsh_in"), sem("w_in")
        x0_in, x_in = sem("x0_in"), sem("x_in")
        ctr_in, cn_in, cr_in = ([sem(f"{n}{q}") for q in range(2)] for n in ("ctx_tr_in", "ctx_n_in", "ctx_rep_in"))
        const = sem("const")
        skipw_ready = sem("skipw_ready")
        s1a, s1b, s1c, s1d = sem("bn1"), sem("mean1"), sem("vareps1"), sem("rstd1")
        v_ready, vc_ready, vt_ps, vt_ready = sem("v_ready"), sem("vc_ready"), sem("vt_ps"), sem("vt_ready")
        kv0_ready, kv1_ready = sem("kv0_ready"), sem("kv1_ready")
        conv_done, prod_ready, even_done, sum_done = sem("conv_done"), sem("prod_ready"), sem("even_done"), sem("sum_done")
        g_done, skip_ready, xa_ready, resid_ready = sem("g_done"), sem("skip_ready"), sem("xa_ready"), sem("resid_ready")
        s2a, s2b, s2c, s2d, s2e = sem("bn2"), sem("mean2"), sem("vareps2"), sem("rstd2"), sem("shift2")
        xn_ready, row_ready, xt_done, xnt_ready, xnt_all = (
            sem("xn_ready"), sem("row_ready"), sem("xt_done"), sem("xnt_ready"), sem("xnt_all"))
        logits_done = sem("logits_done")
        r = sem("route_step")
        mx_sub, exp_done, sel_ready, rank_done, slots_ready, map_ready = (
            sem("mx_sub"), sem("exp_done"), sem("sel_ready"), sem("rank_done"), sem("slots_ready"), sem("map_ready"))
        scattered, padded = sem("scattered"), sem("padded")
        rows_in = [sem("rows_in0"), sem("rows_in1")]
        xtr_ps, xtr_ready, up_done, silu_done, hid_ready, ht_done, htr_ready, dn_done = (
            sem("xtr_ps"), sem("xtr_ready"), sem("up_done"), sem("silu_done"), sem("hid_ready"), sem("ht_done"),
            sem("htr_ready"), sem("dn_done"))
        gate_ready, dest_ready, z_added, y_ready = sem("gate_ready"), sem("dest_ready"), sem("z_added"), sem("y_ready")
        y_sent = [sem("y_sent0"), sem("y_sent1")]
        fin_in = [sem("fin_in0"), sem("fin_in1")]
        fa, fb, fc, fo = sem("fin_a"), sem("fin_b"), sem("fin_c"), sem("fin_o")
        out_sent = [sem("out_sent0"), sem("out_sent1")]

        block = ctx.enter_context(nc.Block())

        def v_forward(q):
            part = v[:, q, :]
            return bass.AP(part.tensor, part.offset + P - 1, [list(part.ap[0]), [P, LB], [-1, P]])

        def at_least(eng, s, n):
            if isinstance(n, int) and n <= 0:
                return
            eng.wait_ge(s, n)

        def part(eng):
            eng.sem_inc(wait_taken, 1)

        def units(eng, step):
            step(0, 0, 1, True, False)
            step(1, 1, 2, False, False)
            with eng.Fori(1, UNITS // 2 - 1) as it:
                step(it * 2, 0, it + 1, False, False)
                step(it * 2 + 1, 1, it + 2, False, False)
            step(UNITS - 2, 0, UNITS // 2, False, False)
            step(UNITS - 1, 1, UNITS // 2 + 1, False, True)

        C_IDENT, C_BLOCKS, C_SUM, C_ALL = 3, 6, 7 + 2 * C, 7 + 2 * C + 11

        @block.sync
        def _(sp):
            def load(u, q):
                late = not (isinstance(u, int) and u < 2)
                if late:
                    sp.wait_ge(kv0_ready, u - 1)
                    sp.wait_ge(kv1_ready, u - 1)
                sp.dma_start(ctx_tr[:, q, :, :].rearrange("p b n -> p (b n)"),
                             ctxt_d[bass.ds(u, 1)].rearrange("a p n -> (a p) n")).then_inc(ctr_in[q], 16)
                if late:
                    sp.wait_ge(skip_ready, u - 1)
                    sp.wait_ge(vc_ready, u - 1)
                sp.dma_start(ctx_n[:, q, :], ctx_d[bass.ds(u, 1)].rearrange("a p l -> (a p) l")).then_inc(cn_in[q], 16)
                if late:
                    sp.wait_ge(prod_ready, (u - 1) * 4)
                src = ctxr_d[bass.ds(u, 1)].rearrange("a g n -> (a g) n")
                src = src.unsqueeze(1).to_broadcast([2 * C, C, HH * L])
                sp.dma_start(ctx_rep[:, q, :, :].rearrange("p h l -> p (h l)"), src).then_inc(cr_in[q], 16)

            sp.dma_start(resid[:, 0, :], x_d[0]).then_inc(x0_in, 16)
            sp.wait_ge(k_zero, 1)
            sp.dma_start(kpad[:, P - 1:P - 1 + L], k_d).then_inc(k_in, 16)
            for q in range(2):
                for hh in range(HH):
                    head = bias_d[(q * HH + hh) * C:(q * HH + hh + 1) * C]
                    sp.dma_start(bias_c[hh * 2 * C:(hh + 1) * 2 * C, q:q + 1],
                                 bass.AP(head.tensor, head.offset, [[0, 2], [1, C], [1, 1]])).then_inc(bias_in, 16)
            sp.wait_ge(k_in, 16)
            sp.dma_start(kpad_d, kpad).then_inc(k_out, 16)
            load(0, 0)
            sp.wait_ge(k_out, 16)
            first = kpad_d[0:H, 0:L]
            window = bass.AP(first.tensor, first.offset, [[1, P], [3 * P, H], [1, L]])
            sp.dma_start(toep[:], window).then_inc(toep_in, 16)
            sp.dma_start(resid[:, 1:, :], x_d[1:].rearrange("u p l -> p u l")).then_inc(x_in, 16)
            load(1, 1)
            sp.dma_start(wg[:], wg_d).then_inc(wg_in, 16)
            with sp.Fori(1, UNITS // 2) as it:
                load(it * 2, 0)
                load(it * 2 + 1, 1)
            sp.wait_ge(map_ready, 1)
            with sp.Fori(0, E) as e:
                at = sp.value_load(pad_at[0:1, bass.ds(e, 1)], min_val=0, max_val=E * REGION)
                sp.dma_start(rows_d[bass.ds(at, P)], pad_row[:, 0, :]).then_inc(padded, 16)
            sp.dma_start(rows_d[E * REGION:E * REGION + P], pad_row[:, 1, :]).then_inc(padded, 16)
            sp.wait_ge(padded, 16 * (E + 1))
            sp.wait_ge(scattered, 16 * UNITS * TOPK)

            def gather(t, q):
                w = t + SHARED
                if not (isinstance(t, int) and t < 2):
                    sp.wait_ge(xtr_ps, t - 1)
                    sp.wait_ge(dest_ready, t - 1)
                at = sp.value_load(tile_row[0:1, bass.ds(t, 1)], min_val=0, max_val=E * REGION)
                sp.dma_start(xg[q], rows_d[bass.ds(at, P)]).then_inc(rows_in[q], 16)

            gather(0, 0)
            gather(1, 1)
            with sp.Fori(1, TILES // 2) as it:
                gather(it * 2, 0)
                gather(it * 2 + 1, 1)
            sp.wait_ge(y_sent[0], 16 * (TILES // 2))
            sp.wait_ge(y_sent[1], 16 * (TILES // 2))
            y_v = y_d[0:TOPK * TOK].rearrange("(k n) l -> n k l", k=TOPK)

            def final(u, q, first=False):
                if not first:
                    sp.wait_ge(fa, u - 1)
                    sp.wait_ge(fb, u - 1)
                sp.dma_start(fin[q], y_v[bass.ds(u * P, P)]).then_inc(fin_in[q], 16)

            def store(u, q):
                sp.wait_ge(fo, u + 1)
                sp.dma_start(out_d[bass.ds(u, 1)].rearrange("a p l -> (a p) l"), fin_o[q]).then_inc(out_sent[q], 16)

            final(0, 0, True)
            final(1, 1, True)
            with sp.Fori(1, UNITS // 2) as it:
                final(it * 2, 0)
                store(it * 2 - 2, 0)
                final(it * 2 + 1, 1)
                store(it * 2 - 1, 1)
            store(UNITS - 2, 0)
            store(UNITS - 1, 1)
            sp.wait_ge(out_sent[0], 16 * (UNITS // 2))
            sp.wait_ge(out_sent[1], 16 * (UNITS // 2))

        @block.scalar
        def _(act):
            act.dma_start(w13[:, E:, :, :], w13_d[:, E:, :, :]).then_inc(wsh_in, 16)
            act.dma_start(w2[:, E:, :, :], w2_d[:, E:, :, :]).then_inc(wsh_in, 16)
            act.dma_start(w13[:, 0:E, :, :], w13_d[:, 0:E, :, :]).then_inc(w_in, 16)
            act.dma_start(w2[:, 0:E, :, :], w2_d[:, 0:E, :, :]).then_inc(w_in, 16)

            def copy_v(u, q):
                act.wait_ge(vt_ps, u + 1)
                if not (isinstance(u, int) and u < 2):
                    act.wait_ge(kv0_ready, u - 1)
                    act.wait_ge(kv1_ready, u - 1)
                nc.scalar.activation(v_tr[:, q, :, :], tr_ps, ACT.Copy).then_inc(vt_ready, 1)

            def normal(u, q):
                act.wait_ge(s2e, u + 1)
                if not (isinstance(u, int) and u < 2):
                    act.wait_ge(xt_done, u - 1)
                part(act)
                nc.scalar.activation(xn[:, q, :], resid[:, bass.ds(u, 1), :].rearrange("p a l -> p (a l)"),
                                     ACT.Identity, bias=st2[:, q, 10:11], scale=st2[:, q, 9:10]).then_inc(xn_ready, 1)
                nc.scalar.activation(rows[:, bass.ds(u, 1), 0:L].rearrange("p a l -> p (a l)"),
                                     resid[:, bass.ds(u, 1), :].rearrange("p a l -> p (a l)"),
                                     ACT.Identity, bias=st2[:, q, 10:11], scale=st2[:, q, 9:10]).then_inc(row_ready, 1)

            def copy_xn(u, q):
                act.wait_ge(xt_done, u + 1)
                if not (isinstance(u, int) and u < 2):
                    act.wait_ge(logits_done, u - 1)
                nc.scalar.activation(xn_tr[:, q, :, :], tr_ps, ACT.Copy).then_inc(xnt_ready, 1)
                nc.scalar.activation(xn_tr_all[:, bass.ds(u, 1), :, :].rearrange("p a b n -> p (a b) n"), tr_ps,
                                     ACT.Copy).then_inc(xnt_all, 1)

            def step(u, q, landed, first, last):
                if not last:
                    copy_v(u + 1, 1 - q)
                if not first:
                    normal(u - 1, 1 - q)
                    copy_xn(u - 1, 1 - q)

            copy_v(0, 0)
            units(act, step)
            normal(UNITS - 1, 1)
            copy_xn(UNITS - 1, 1)

            act.wait_ge(mx_sub, 1)
            nc.scalar.activation(rt[:, 1, :], rt[:, 0, :], ACT.Exp).then_inc(exp_done, 1)
            nc.scalar.preload_act_table(ACT.Silu)

            def src_tr(w, p, tile=None):
                if not (isinstance(w, int) and w < 2):
                    act.wait_ge(up_done, w - 1)
                if tile is None:
                    act.wait_ge(xtr_ps, w - SHARED + 1)
                    src = xt_ps[p]
                else:
                    src = xn_tr_all[:, bass.ds(tile, 1), :, :].rearrange("p a b n -> p (a b) n")
                part(act)
                nc.scalar.activation(x_tr[p], src, ACT.Copy).then_inc(xtr_ready, 1)

            def silu(w, p):
                act.wait_ge(up_done, w + 1)
                if not (isinstance(w, int) and w < 2):
                    act.wait_ge(hid_ready, w - 1)
                nc.scalar.activation(act1[p], up_ps[p][:, 0:INTER], ACT.Silu).then_inc(silu_done, 1)

            def store_y(w, p, sent):
                act.wait_ge(dn_done, w + 1)
                at_least(act, y_sent[p], sent * 16)
                nc.scalar.activation(y_sb[p], dn_ps[p], ACT.Copy).then_inc(y_ready, 1)

            act.wait_ge(xnt_all, UNITS)
            act.wait_ge(conv_done, 4 * UNITS)
            src_tr(0, 0, 0)
            silu(0, 0)
            src_tr(1, 1, 0)
            with act.Fori(1, UNITS) as it:
                silu(it * 2 - 1, 1)
                src_tr(it * 2, 0, it)
                silu(it * 2, 0)
                src_tr(it * 2 + 1, 1, it)
            silu(SHARED - 1, 1)
            src_tr(SHARED, 0)
            silu(SHARED, 0)
            src_tr(SHARED + 1, 1)
            silu(SHARED + 1, 1)
            src_tr(SHARED + 2, 0)
            silu(SHARED + 2, 0)
            src_tr(SHARED + 3, 1)
            store_y(SHARED, 0, 0)
            with act.Fori(1, TILES // 2 - 1) as it:
                silu(it * 2 + (SHARED + 1), 1)
                src_tr(it * 2 + (SHARED + 2), 0)
                store_y(it * 2 + (SHARED - 1), 1, it - 1)
                silu(it * 2 + (SHARED + 2), 0)
                src_tr(it * 2 + (SHARED + 3), 1)
                store_y(it * 2 + SHARED, 0, it)
            silu(STEPS - 1, 1)
            store_y(STEPS - 3, 1, TILES // 2 - 2)
            store_y(STEPS - 2, 0, TILES // 2 - 1)
            store_y(STEPS - 1, 1, TILES // 2 - 1)

        @block.gpsimd
        def _(pool):
            n = [0]

            def done(ins):
                n[0] += 1
                ins.then_inc(const, 1)
                pool.wait_ge(const, n[0])

            nc.gpsimd.memset(kpad, 0.0).then_inc(k_zero, 1)
            done(nc.gpsimd.memset(neg_half[:], -0.5))
            done(nc.gpsimd.memset(ident[:], 0.0))
            done(nc.gpsimd.affine_select(out=ident[:], in_=ident[:], compare_op=ALU.not_equal, fill=1.0, base=0,
                                         pattern=[[-1, P]], channel_multiplier=1))
            done(nc.gpsimd.memset(blocks[:], 1.0))
            bv = blocks[:].rearrange("p (n j) -> p n j", j=C)
            done(nc.gpsimd.affine_select(out=bv, in_=bv, compare_op=ALU.is_ge, fill=0.0, base=0,
                                         pattern=[[-C, P // C], [0, C]], channel_multiplier=1))
            done(nc.gpsimd.affine_select(out=bv, in_=bv, compare_op=ALU.is_ge, fill=0.0, base=C - 1,
                                         pattern=[[C, P // C], [0, C]], channel_multiplier=-1))
            done(nc.gpsimd.memset(sum_i[:], 0.0))

            def v_stats(u, q):
                pool.wait_ge(s1b, u + 1)
                part(pool)
                nc.gpsimd.tensor_scalar(st1[:, q, 8:9], st1[:, q, 7:8], EPS, None, ALU.add).then_inc(s1c, 1)
                pool.wait_ge(s1c, u + 1)
                nc.gpsimd.tensor_tensor(st1[:, q, 9:10], st1[:, q, 8:9], neg_half[:], ALU.pow).then_inc(s1d, 1)

            v_stats(0, 0)
            for i in range(C):
                for par in range(2):
                    sv = sum_i[:, par, 16 * par:16 * par + 16].rearrange("p (b j) -> p b j", j=C)
                    done(nc.gpsimd.affine_select(out=sv, in_=sv, compare_op=ALU.not_equal, fill=1.0, base=-C * i,
                                                 pattern=[[-64, 2], [-1, C]], channel_multiplier=1))
            assert n[0] == 7 + 2 * C

            def v_work(u, q, landed):
                pool.wait_ge(v_ready, u + 1)
                if not (isinstance(u, int) and u < 2):
                    pool.wait_ge(resid_ready, u - 1)
                pool.wait_ge(cn_in[q], landed * 16)
                nc.gpsimd.tensor_tensor(vc[:, q, :].rearrange("p (b n) -> p b n", b=LB), v_forward(q),
                                        ctx_n[:, q, :].rearrange("p (b n) -> p b n", b=LB), ALU.mult).then_inc(vc_ready, 1)
                pool.wait_ge(vt_ready, u + 1)
                if not (isinstance(u, int) and u < 2):
                    pool.wait_ge(conv_done, 4 * (u - 1))
                pool.wait_ge(ctr_in[q], landed * 16)
                nc.gpsimd.tensor_tensor(
                    kv[:, q, 1, :].rearrange("p (g i j) -> p g i j", i=C, j=C),
                    v_tr[:, q, 1, :].rearrange("p (g i) -> p g i", i=C).unsqueeze(3).to_broadcast([P, 2 * HH, C, C]),
                    ctx_tr[:, q, 1, :].rearrange("p (g j) -> p g j", j=C).unsqueeze(2).to_broadcast([P, 2 * HH, C, C]),
                    ALU.mult).then_inc(kv1_ready, 1)

            def x_work(u, q):
                pool.wait_ge(xa_ready, u + 1)
                pool.wait_ge(skip_ready, u + 1)
                rv = resid[:, bass.ds(u, 1), :].rearrange("p a l -> p (a l)")
                nc.gpsimd.tensor_tensor(rv, rv, skip[:, q, :], ALU.add).then_inc(resid_ready, 1)
                pool.wait_ge(s2b, u + 1)
                part(pool)
                nc.gpsimd.tensor_scalar(st2[:, q, 8:9], st2[:, q, 7:8], EPS, None, ALU.add).then_inc(s2c, 1)
                pool.wait_ge(s2c, u + 1)
                nc.gpsimd.tensor_tensor(st2[:, q, 9:10], st2[:, q, 8:9], neg_half[:], ALU.pow).then_inc(s2d, 1)

            def step(u, q, landed, first, last):
                if not last:
                    v_stats(u + 1, 1 - q)
                if not first:
                    x_work(u - 1, 1 - q)
                if not last:
                    v_work(u + 1, 1 - q, landed)

            v_work(0, 0, 1)
            units(pool, step)
            x_work(UNITS - 1, 1)

            done(nc.gpsimd.memset(ones[:], 1.0))
            done(nc.gpsimd.affine_select(out=before[:], in_=ones[:], compare_op=ALU.is_gt, fill=0.0, base=0,
                                         pattern=[[1, P]], channel_multiplier=-1))
            done(nc.gpsimd.memset(low[:], 1.0))
            done(nc.gpsimd.affine_select(out=low[:], in_=low[:], compare_op=ALU.is_gt, fill=0.0, base=0,
                                         pattern=[[1, G], [-1, G]], channel_multiplier=0))
            exact = dict(allow_small_or_imprecise_dtypes=True)
            done(nc.gpsimd.iota(io_e[:], [[1, E]], base=0, channel_multiplier=0, **exact))
            done(nc.gpsimd.iota(io_tok[:], [[P, UNITS], [0, E]], base=0, channel_multiplier=1, **exact))
            done(nc.gpsimd.iota(io_reg[:], [[REGION, E]], base=0, channel_multiplier=0, **exact))
            done(nc.gpsimd.iota(io_j[:], [[P, E]], base=0, channel_multiplier=0, **exact))
            done(nc.gpsimd.iota(io_t[:], [[1, TILES]], base=0, channel_multiplier=0, **exact))
            done(nc.gpsimd.memset(pad_row[:, :, 0:L + E], 0.0))
            done(nc.gpsimd.iota(pad_row[:, :, L + E:], [[E * P, 2], [P, E]], base=TOPK * TOK, channel_multiplier=1,
                                **exact))

            pool.wait_ge(row_ready, UNITS)
            pool.wait_ge(slots_ready, 1)
            for u in range(UNITS):
                for k in range(TOPK):
                    pool.indirect_dma_start(
                        rows_d, bass.IndirectOffsetOnAxis(ap=slot_i[:, u, k:k + 1].bitcast(U32), axis=0),
                        rows[:, u, :], None).then_inc(scattered, 16)

            def send(t, q):
                pool.wait_ge(y_ready, t + 1)
                pool.wait_ge(dest_ready, t + 1)
                part(pool)
                pool.indirect_dma_start(
                    y_d, bass.IndirectOffsetOnAxis(ap=dest_i[q][:, 0:1].bitcast(U32), axis=0),
                    y_sb[q], None).then_inc(y_sent[q], 16)

            with pool.Fori(0, TILES // 2) as it:
                send(it * 2, 0)
                send(it * 2 + 1, 1)

            def final(u, q, landed):
                pool.wait_ge(fin_in[q], landed * 16)
                if not (isinstance(u, int) and u < 2):
                    pool.wait_ge(fo, u - 1)
                nc.gpsimd.tensor_tensor(fin_b[q], fin[q][:, 3, :],
                                        resid[:, bass.ds(u, 1), :].rearrange("p a l -> p (a l)"),
                                        ALU.add).then_inc(fb, 1)

            pool.wait_ge(z_added, UNITS)
            final(0, 0, 1)
            final(1, 1, 1)
            with pool.Fori(1, UNITS // 2) as it:
                final(it * 2, 0, it + 1)
                final(it * 2 + 1, 1, it + 1)

        @block.vector
        def _(dve):
            def tile(u):
                return resid[:, bass.ds(u, 1), :].rearrange("p a l -> p (a l)")

            def stats1(u, q):
                if isinstance(u, int) and u == 0:
                    dve.wait_ge(x0_in, 16)
                else:
                    dve.wait_ge(x_in, 16)
                nc.vector.bn_stats(st1[:, q, 0:6], tile(u)).then_inc(s1a, 1)
                dve.wait_ge(s1a, u + 1)
                part(dve)
                nc.vector.bn_aggr(st1[:, q, 6:8], st1[:, q, 0:6]).then_inc(s1b, 1)

            def norm1(u, q):
                dve.wait_ge(s1d, u + 1)
                if not (isinstance(u, int) and u < 2):
                    dve.wait_ge(vt_ps, u - 1)
                    dve.wait_ge(vc_ready, u - 1)
                nc.vector.tensor_scalar(v_forward(q), tile(u).rearrange("p (b n) -> p b n", b=LB), st1[:, q, 6:7], st1[:, q, 9:10],
                                        ALU.subtract, ALU.mult).then_inc(v_ready, 1)

            def kv_block0(u, q, landed):
                dve.wait_ge(ctr_in[q], landed * 16)
                dve.wait_ge(vt_ready, u + 1)
                if not (isinstance(u, int) and u < 2):
                    dve.wait_ge(conv_done, 4 * (u - 1))
                nc.vector.tensor_tensor(
                    kv[:, q, 0, :].rearrange("p (g i j) -> p g i j", i=C, j=C),
                    v_tr[:, q, 0, :].rearrange("p (g i) -> p g i", i=C).unsqueeze(3).to_broadcast([P, 2 * HH, C, C]),
                    ctx_tr[:, q, 0, :].rearrange("p (g j) -> p g j", j=C).unsqueeze(2).to_broadcast([P, 2 * HH, C, C]),
                    ALU.mult).then_inc(kv0_ready, 1)

            def product(u, q, g, landed, first):
                dve.wait_ge(conv_done, 4 * u + g + 1)
                if g == 0:
                    dve.wait_ge(cr_in[q], (landed - q) * 16)
                if not first:
                    dve.wait_ge(even_done if g < 2 else sum_done, u)
                h0 = HEADS[g]
                nc.vector.tensor_tensor(prod[:, g, :, :], y_ps[g], ctx_rep[:, q, h0:h0 + 3:2, :],
                                        ALU.mult).then_inc(prod_ready, 1)

            def add_x(u, q):
                dve.wait_ge(sum_done, u + 1)
                nc.vector.tensor_tensor(tile(u), o_ps, tile(u), ALU.add).then_inc(xa_ready, 1)

            def skip_term(u, q):
                dve.wait_ge(g_done, u + 1)
                if not (isinstance(u, int) and u < 2):
                    dve.wait_ge(resid_ready, u - 1)
                nc.vector.tensor_tensor(skip[:, q, :], g_ps, ctx_n[:, q, :], ALU.mult).then_inc(skip_ready, 1)

            def stats2(u, q):
                dve.wait_ge(resid_ready, u + 1)
                part(dve)
                nc.vector.bn_stats(st2[:, q, 0:6], tile(u)).then_inc(s2a, 1)
                dve.wait_ge(s2a, u + 1)
                if not (isinstance(u, int) and u < 2):
                    dve.wait_ge(row_ready, u - 1)
                part(dve)
                nc.vector.bn_aggr(st2[:, q, 6:8], st2[:, q, 0:6]).then_inc(s2b, 1)

            def shift2(u, q):
                dve.wait_ge(s2d, u + 1)
                nc.vector.scalar_tensor_tensor(st2[:, q, 10:11], st2[:, q, 6:7], -1.0, st2[:, q, 9:10],
                                               ALU.mult, ALU.mult).then_inc(s2e, 1)

            def step(u, q, landed, first, last):
                if not last:
                    stats1(u + 1, 1 - q)
                product(u, q, 0, landed, first)
                if not last:
                    norm1(u + 1, 1 - q)
                if not first:
                    add_x(u - 1, 1 - q)
                product(u, q, 1, landed, first)
                skip_term(u, q)
                if not first:
                    stats2(u - 1, 1 - q)
                product(u, q, 2, landed, first)
                if not first:
                    shift2(u - 1, 1 - q)
                if not last:
                    kv_block0(u + 1, 1 - q, landed)
                product(u, q, 3, landed, first)

            stats1(0, 0)
            norm1(0, 0)
            kv_block0(0, 0, 1)
            dve.wait_ge(bias_in, 16 * 2 * HH)
            dve.wait_ge(const, C_BLOCKS)
            for q in range(2):
                nc.vector.tensor_scalar(skip_w[:, q, :], blocks[:], bias_c[:, q:q + 1], None, ALU.mult
                                        ).then_inc(skipw_ready, 1)
            units(dve, step)
            add_x(UNITS - 1, 1)
            stats2(UNITS - 1, 1)
            shift2(UNITS - 1, 1)

            n = [0]

            def then(ins):
                n[0] += 1
                ins.then_inc(r, 1)
                dve.wait_ge(r, n[0])

            te = lambda i: rt[:, i, :].rearrange("p (t e) -> p t e", e=E)
            lg = logit_ps.rearrange("p (t e) -> p t e", e=E)
            mx = rt[:, 2, 0:UNITS]
            dve.wait_ge(logits_done, UNITS)
            then(nc.vector.tensor_reduce(mx, lg, AX_X, ALU.max))
            nc.vector.tensor_tensor(te(0), lg, mx.unsqueeze(2).to_broadcast([P, UNITS, E]),
                                    ALU.subtract).then_inc(mx_sub, 1)
            dve.wait_ge(exp_done, 1)
            then(nc.vector.tensor_reduce(rt[:, 2, 16:32], te(1), AX_X, ALU.add))
            then(nc.vector.reciprocal(rt[:, 2, 32:48], rt[:, 2, 16:32]))
            then(nc.vector.tensor_tensor(te(3), te(1), rt[:, 2, 32:48].unsqueeze(2).to_broadcast([P, UNITS, E]),
                                         ALU.mult))
            gm = rt[:, 2, 64:64 + UNITS * G].rearrange("p (t g) -> p t g", g=G)
            then(nc.vector.tensor_reduce(rt[:, 2, 64:64 + UNITS * G], rt[:, 3, :].rearrange("p (n i) -> p n i", i=GE),
                                         AX_X, ALU.max))
            other = gm.unsqueeze(2).to_broadcast([P, UNITS, G, G])
            own = gm.unsqueeze(3).to_broadcast([P, UNITS, G, G])
            tgg = lambda i: rt[:, i, :].rearrange("p (t g o) -> p t g o", g=G, o=G)
            then(nc.vector.tensor_tensor(tgg(4), other, own, ALU.is_equal))
            then(nc.vector.tensor_tensor(tgg(5), other, own, ALU.is_gt))
            dve.wait_ge(const, C_ALL)
            then(nc.vector.tensor_tensor(tgg(4), tgg(4), low[:].unsqueeze(1).to_broadcast([P, UNITS, G, G]), ALU.mult))
            then(nc.vector.tensor_tensor(tgg(5), tgg(4), tgg(5), ALU.add))
            then(nc.vector.tensor_reduce(rt[:, 2, 128:192], rt[:, 5, :].rearrange("p (n o) -> p n o", o=G),
                                         AX_X, ALU.add))
            then(nc.vector.tensor_scalar(rt[:, 2, 192:256], rt[:, 2, 128:192], TOP_G - 0.5, None, ALU.is_lt))
            kept = rt[:, 2, 192:256].unsqueeze(2).to_broadcast([P, UNITS * G, GE])
            ng = lambda i: rt[:, i, :].rearrange("p (n i) -> p n i", i=GE)
            then(nc.vector.tensor_tensor(ng(4), ng(3), kept, ALU.mult))
            then(nc.vector.scalar_tensor_tensor(ng(5), kept, -1.0, ng(4), ALU.add, ALU.add))
            for t in range(UNITS):
                last = nc.vector.max(top8[:, t, :], te(5)[:, t, :])
            then(last)
            for t in range(UNITS):
                last = nc.vector.max_index(top_i[:, t, :], top8[:, t, :], te(5)[:, t, :])
            then(last)
            idx_f = rt[:, 6, 0:UNITS * TOPK].rearrange("p (t k) -> p t k", k=TOPK)
            then(nc.vector.tensor_copy(idx_f, top_i[:, :, 0:TOPK]))
            then(nc.vector.tensor_tensor(onehot, idx_f.unsqueeze(3).to_broadcast([P, UNITS, TOPK, E]),
                                         io_e[:].unsqueeze(1).unsqueeze(1).to_broadcast([P, UNITS, TOPK, E]),
                                         ALU.is_equal))
            then(nc.vector.tensor_tensor(te(4), onehot[:, :, 0, :], onehot[:, :, 1, :], ALU.add))
            then(nc.vector.tensor_tensor(te(6), onehot[:, :, 2, :], onehot[:, :, 3, :], ALU.add))
            then(nc.vector.tensor_tensor(te(7), te(4), te(6), ALU.add))
            nc.vector.tensor_copy(sel_bf[:], te(7)).then_inc(sel_ready, 1)
            then(nc.vector.tensor_tensor(rows[:, :, L:L + E], te(7), te(3), ALU.mult))
            then(nc.vector.scalar_tensor_tensor(te(8), onehot[:, :, 2, :], 2.0, onehot[:, :, 1, :], ALU.mult, ALU.add))
            then(nc.vector.scalar_tensor_tensor(te(9), onehot[:, :, 3, :], 3.0, te(8), ALU.mult, ALU.add))
            then(nc.vector.scalar_tensor_tensor(rows[:, :, L + E:], te(9), float(TOK), io_tok[:], ALU.mult, ALU.add))
            dve.wait_ge(rank_done, 1)
            then(nc.vector.tensor_tensor(te(8), rank_ps, io_reg[:].unsqueeze(1).to_broadcast([P, UNITS, E]), ALU.add))
            wv = wide.rearrange("p (t k e) -> p t k e", k=TOPK, e=E)
            then(nc.vector.tensor_tensor(wv, onehot, te(8).unsqueeze(2).to_broadcast([P, UNITS, TOPK, E]), ALU.mult))
            then(nc.vector.tensor_reduce(rt[:, 6, 64:128], wide.rearrange("p (n e) -> p n e", e=E), AX_X, ALU.add))
            nc.vector.tensor_copy(slot_i[:].rearrange("p t k -> p (t k)"), rt[:, 6, 64:128]).then_inc(slots_ready, 1)
            cnt, tiles_e = meta[:, 0, 0:E], meta[:, 0, E:2 * E]
            then(nc.vector.tensor_reduce(cnt, count_ps[0:1].rearrange("p t e -> p e t"), AX_X, ALU.add))
            jj = wide_m[:, 0:E, :]
            then(nc.vector.tensor_tensor(jj, cnt.unsqueeze(2).to_broadcast([1, E, E]),
                                         io_j[:].unsqueeze(1).to_broadcast([1, E, E]), ALU.is_gt))
            then(nc.vector.tensor_reduce(tiles_e, jj, AX_X, ALU.add))
            upto = [meta[:, 1, 0:E], meta[:, 1, E:2 * E]]
            then(nc.vector.tensor_copy(upto[0], tiles_e))
            for i, sh in enumerate((1, 2, 4, 8)):
                a, b = upto[i % 2], upto[1 - i % 2]
                then(nc.vector.tensor_copy(b[:, 0:sh], a[:, 0:sh]))
                then(nc.vector.tensor_tensor(b[:, sh:], a[:, sh:], a[:, 0:E - sh], ALU.add))
            then(nc.vector.tensor_tensor(wide_m, io_t[:].unsqueeze(2).to_broadcast([1, TILES, E]),
                                         upto[0].unsqueeze(1).to_broadcast([1, TILES, E]), ALU.is_ge))
            then(nc.vector.tensor_reduce(meta[:, 2, :], wide_m, AX_X, ALU.add))
            then(nc.vector.tensor_tensor(wide_m, wide_m, tiles_e.unsqueeze(1).to_broadcast([1, TILES, E]), ALU.mult))
            then(nc.vector.tensor_reduce(meta[:, 3, :], wide_m, AX_X, ALU.add))
            then(nc.vector.tensor_tensor(meta[:, 4, :], io_t[:], meta[:, 3, :], ALU.subtract))
            then(nc.vector.tensor_scalar(meta[:, 5, :], meta[:, 2, :], float(REGION), None, ALU.mult))
            then(nc.vector.scalar_tensor_tensor(meta[:, 3, :], meta[:, 4, :], float(P), meta[:, 5, :],
                                                ALU.mult, ALU.add))
            then(nc.vector.tensor_scalar(tile_row[:], meta[:, 3, :], float(E * REGION), None, ALU.min))
            then(nc.vector.tensor_scalar(meta[:, 5, :], meta[:, 2, :], E - 0.5, None, ALU.is_gt))
            then(nc.vector.scalar_tensor_tensor(meta[:, 3, :], meta[:, 4, :], float(-E), meta[:, 5, :],
                                                ALU.add, ALU.mult))
            then(nc.vector.tensor_tensor(tile_e[:], meta[:, 3, :], meta[:, 2, :], ALU.add))
            nc.vector.tensor_tensor(pad_at[:], cnt, io_reg[0:1, :], ALU.add).then_inc(map_ready, 1)

            def hidden(w, p, t=None):
                dve.wait_ge(silu_done, w + 1)
                if not (isinstance(w, int) and w < 2):
                    dve.wait_ge(ht_done, w - 1)
                if t is None:
                    nc.vector.tensor_tensor(hid[p], act1[p], up_ps[p][:, INTER:], ALU.mult).then_inc(hid_ready, 1)
                else:
                    dve.wait_ge(gate_ready, t + 1)
                    nc.vector.scalar_tensor_tensor(hid[p], act1[p], gate_c[p][:, 0:1], up_ps[p][:, INTER:],
                                                   ALU.mult, ALU.mult).then_inc(hid_ready, 1)

            def copy_h(w, p):
                dve.wait_ge(ht_done, w + 1)
                if not (isinstance(w, int) and w < 2):
                    dve.wait_ge(dn_done, w - 1)
                nc.vector.tensor_copy(hid_tr[p], ht_ps[p]).then_inc(htr_ready, 1)

            def add_z(t):
                dve.wait_ge(dn_done, t * 2 + 2)
                rv = resid[:, bass.ds(t, 1), :].rearrange("p a l -> p (a l)")
                nc.vector.tensor_tensor(rv, dn_ps[0], rv, ALU.add).then_inc(z_added, 1)

            def take(t, p, pair):
                dve.wait_ge(rows_in[p], pair * 16 + 16)
                if not isinstance(t, int):
                    dve.wait_ge(hid_ready, t + SHARED - 1)
                    dve.wait_ge(y_sent[p], pair * 16)
                e = dve.value_load(tile_e[0:1, bass.ds(t, 1)], min_val=0, max_val=E - 1)
                nc.vector.tensor_copy(gate_c[p][:, 0:1], xg[p][:, bass.ds(e + L, 1)]).then_inc(gate_ready, 1)
                nc.vector.tensor_copy(dest_i[p][:, 0:1], xg[p][:, bass.ds(e + (L + E), 1)]).then_inc(dest_ready, 1)

            hidden(0, 0)
            copy_h(0, 0)
            hidden(1, 1)
            with dve.Fori(1, UNITS) as it:
                copy_h(it * 2 - 1, 1)
                hidden(it * 2, 0)
                copy_h(it * 2, 0)
                hidden(it * 2 + 1, 1)
                add_z(it - 1)
            copy_h(SHARED - 1, 1)
            take(0, 0, 0)
            hidden(SHARED, 0, 0)
            copy_h(SHARED, 0)
            take(1, 1, 0)
            hidden(SHARED + 1, 1, 1)
            add_z(UNITS - 1)
            with dve.Fori(1, TILES // 2) as it:
                copy_h(it * 2 + (SHARED - 1), 1)
                take(it * 2, 0, it)
                hidden(it * 2 + SHARED, 0, it * 2)
                copy_h(it * 2 + SHARED, 0)
                take(it * 2 + 1, 1, it)
                hidden(it * 2 + (SHARED + 1), 1, it * 2 + 1)
            copy_h(STEPS - 1, 1)

            def final(u, q, pair):
                dve.wait_ge(fin_in[q], pair * 16 + 16)
                nc.vector.tensor_tensor(fin_a[q], fin[q][:, 0, :], fin[q][:, 1, :], ALU.add).then_inc(fc, 1)
                dve.wait_ge(fc, u + 1)
                nc.vector.tensor_tensor(fin_a[q], fin_a[q], fin[q][:, 2, :], ALU.add).then_inc(fa, 1)
                dve.wait_ge(fa, u + 1)
                dve.wait_ge(fb, u + 1)
                at_least(dve, out_sent[q], pair * 16)
                nc.vector.tensor_tensor(fin_o[q], fin_a[q], fin_b[q], ALU.add).then_inc(fo, 1)

            final(0, 0, 0)
            final(1, 1, 0)
            with dve.Fori(1, UNITS // 2) as it:
                final(it * 2, 0, it)
                final(it * 2 + 1, 1, it)

        @block.tensor
        def _(pe):
            def transpose_v(u, q):
                pe.wait_ge(v_ready, u + 1)
                if not (isinstance(u, int) and u < 3):
                    pe.wait_ge(xnt_all, u - 2)
                for blk in range(LB):
                    last = nc.tensor.transpose(tr_ps[:, blk, :], v[:, q, blk * P:(blk + 1) * P], ident[:])
                last.then_inc(vt_ps, 1)

            def convolve(u, q, g):
                if g == 0:
                    pe.wait_ge(kv0_ready, u + 1)
                    pe.wait_ge(kv1_ready, u + 1)
                if not (isinstance(u, int) and u < 1):
                    pe.wait_ge(prod_ready, u * 4 + (g - 3))
                for s in range(2):
                    h = HEADS[g] + 2 * s
                    nc.tensor.matmul(y_ps[g][:, s, :], kv[:, q, 0, h * P:(h + 1) * P], toep[:, q * HH + h, :],
                                     start=True, stop=False)
                    last = nc.tensor.matmul(y_ps[g][:, s, P:], kv[:, q, 1, h * P:(h + 1) * P],
                                            toep[:, q * HH + h, 0:P], start=False, stop=True)
                last.then_inc(conv_done, 1)

            def sums(u, par):
                pe.wait_ge(prod_ready, u * 4 + 2 + 2 * par)
                if par == 0 and not (isinstance(u, int) and u < 1):
                    pe.wait_ge(xa_ready, u)
                for c in range(4):
                    last = nc.tensor.matmul(bank[4][32 * c:32 * c + 32, 0:L], sum_i[:, par, :],
                                            prod[:, 2 * par + c // 2, c % 2, :], start=par == 0, stop=par == 1)
                last.then_inc(sum_done if par else even_done, 1)

            def skip_sum(u, q):
                pe.wait_ge(vc_ready, u + 1)
                if not (isinstance(u, int) and u < 1):
                    pe.wait_ge(skip_ready, u)
                nc.tensor.matmul(g_ps, skip_w[:, q, :], vc[:, q, :], start=True, stop=True).then_inc(g_done, 1)

            def router(u, q):
                pe.wait_ge(xn_ready, u + 1)
                if isinstance(u, int) and u + 3 > UNITS:
                    pe.wait_ge(vt_ready, UNITS)
                    at_least(pe, xnt_all, u)
                else:
                    pe.wait_ge(vt_ready, u + 3)
                for blk in range(LB):
                    last = nc.tensor.transpose(tr_ps[:, blk, :], xn[:, q, blk * P:(blk + 1) * P], ident[:])
                last.then_inc(xt_done, 1)
                pe.wait_ge(xnt_ready, u + 1)
                for blk in range(LB):
                    last = nc.tensor.matmul(logit_ps[:, bass.ds(u * E, E)], xn_tr[:, q, blk, :], wg[:, blk, :],
                                            start=blk == 0, stop=blk == LB - 1)
                last.then_inc(logits_done, 1)

            def step(u, q, landed, first, last):
                convolve(u, q, 0)
                if not first:
                    sums(u - 1, 1)
                convolve(u, q, 1)
                skip_sum(u, q)
                if not last:
                    transpose_v(u + 1, 1 - q)
                convolve(u, q, 2)
                sums(u, 0)
                convolve(u, q, 3)
                if not first:
                    router(u - 1, 1 - q)

            pe.wait_ge(const, C_SUM)
            transpose_v(0, 0)
            pe.wait_ge(toep_in, 16)
            pe.wait_ge(skipw_ready, 2)
            pe.wait_ge(wg_in, 16)
            units(pe, step)
            sums(UNITS - 1, 1)
            router(UNITS - 1, 1)

            pe.wait_ge(sel_ready, 1)
            pe.wait_ge(xnt_all, UNITS)
            nc.tensor.matmul(count_ps, ones[:], sel_bf[:], start=True, stop=True)
            nc.tensor.matmul(rank_ps, before[:], sel_bf[:], start=True, stop=False)
            for t in range(UNITS - 1):
                last = nc.tensor.matmul(rank_ps[:, t + 1:, :], ones[:],
                                        sel_bf[:, t:t + 1, :].to_broadcast([P, UNITS - 1 - t, E]),
                                        start=False, stop=t == UNITS - 2)
            last.then_inc(rank_done, 1)

            def expert(t):
                return pe.value_load(tile_e[0:1, bass.ds(t, 1)], min_val=0, max_val=E - 1)

            def up(w, p, t=None):
                pe.wait_ge(xtr_ready, w + 1)
                if not (isinstance(w, int) and w < 2):
                    pe.wait_ge(hid_ready, w - 1)
                e = E + p if t is None else expert(t)
                for blk in range(LB):
                    last = nc.tensor.matmul(up_ps[p], x_tr[p][:, blk, :],
                                            w13[:, bass.ds(e, 1), blk, :].rearrange("p a n -> p (a n)"),
                                            start=blk == 0, stop=blk == LB - 1)
                last.then_inc(up_done, 1)

            def turn_h(w, p):
                pe.wait_ge(hid_ready, w + 1)
                if not (isinstance(w, int) and w < 2):
                    pe.wait_ge(htr_ready, w - 1)
                for c in range(2):
                    last = nc.tensor.transpose(ht_ps[p][:, c, :], hid[p][:, c * HI:(c + 1) * HI], ident[:])
                last.then_inc(ht_done, 1)

            def turn_x(w, p, landed):
                pe.wait_ge(rows_in[p], landed * 16)
                if not (isinstance(w, int) and w < SHARED + 2):
                    pe.wait_ge(xtr_ready, w - 1)
                for blk in range(LB):
                    last = nc.tensor.transpose(xt_ps[p][:, blk, :], xg[p][:, blk * P:(blk + 1) * P], ident[:])
                last.then_inc(xtr_ps, 1)

            def down_shared(w, p, tile):
                pe.wait_ge(htr_ready, w + 1)
                if p == 0:
                    at_least(pe, z_added, tile)
                for c in range(2):
                    last = nc.tensor.matmul(dn_ps[0], hid_tr[p][:, c, :], w2[:, E + p, c, :],
                                            start=p == 0 and c == 0, stop=p == 1 and c == 1)
                last.then_inc(dn_done, 1)

            def down(w, p, t):
                pe.wait_ge(htr_ready, w + 1)
                if isinstance(t, int) and t < 2:
                    pe.wait_ge(z_added, UNITS)
                else:
                    pe.wait_ge(y_ready, t - 1)
                e = expert(t)
                for c in range(2):
                    last = nc.tensor.matmul(dn_ps[p], hid_tr[p][:, c, :],
                                            w2[:, bass.ds(e, 1), c, :].rearrange("p a n -> p (a n)"),
                                            start=c == 0, stop=c == 1)
                last.then_inc(dn_done, 1)

            pe.wait_ge(wsh_in, 32)
            up(0, 0)
            up(1, 1)
            turn_h(0, 0)
            with pe.Fori(1, UNITS - 1) as it:
                up(it * 2, 0)
                turn_h(it * 2 - 1, 1)
                down_shared(it * 2 - 2, 0, it - 1)
                up(it * 2 + 1, 1)
                turn_h(it * 2, 0)
                down_shared(it * 2 - 1, 1, it - 1)
            up(SHARED - 2, 0)
            turn_h(SHARED - 3, 1)
            down_shared(SHARED - 4, 0, UNITS - 2)
            up(SHARED - 1, 1)
            turn_h(SHARED - 2, 0)
            turn_x(SHARED, 0, 1)
            down_shared(SHARED - 3, 1, UNITS - 2)
            pe.wait_ge(w_in, 32)
            pe.wait_ge(map_ready, 1)
            up(SHARED, 0, 0)
            turn_h(SHARED - 1, 1)
            turn_x(SHARED + 1, 1, 1)
            down_shared(SHARED - 2, 0, UNITS - 1)
            up(SHARED + 1, 1, 1)
            turn_h(SHARED, 0)
            turn_x(SHARED + 2, 0, 2)
            down_shared(SHARED - 1, 1, UNITS - 1)

            def routed_pair(it):
                up(it * 2 + SHARED, 0, it * 2)
                turn_h(it * 2 + (SHARED - 1), 1)
                turn_x(it * 2 + (SHARED + 1), 1, it + 1)
                down(it * 2 + (SHARED - 2), 0, it * 2 - 2)
                up(it * 2 + (SHARED + 1), 1, it * 2 + 1)
                turn_h(it * 2 + SHARED, 0)
                turn_x(it * 2 + (SHARED + 2), 0, it + 2)
                down(it * 2 + (SHARED - 1), 1, it * 2 - 1)

            routed_pair(1)
            with pe.Fori(2, TILES // 2 - 1) as it:
                routed_pair(it)
            up(STEPS - 2, 0, TILES - 2)
            turn_h(STEPS - 3, 1)
            turn_x(STEPS - 1, 1, TILES // 2)
            down(STEPS - 4, 0, TILES - 4)
            up(STEPS - 1, 1, TILES - 1)
            turn_h(STEPS - 2, 0)
            down(STEPS - 3, 1, TILES - 3)
            turn_h(STEPS - 1, 1)
            down(STEPS - 2, 0, TILES - 2)
            down(STEPS - 1, 1, TILES - 1)


def kernel(x, fside_S2_0, ctx_2048, L0_xattn_k, L0_ffn_Wg, L0_ffn_W1, L0_ffn_W3, L0_ffn_W2, L0_ffn_Ws1, L0_ffn_Ws3,
           L0_ffn_Ws2):
    import concourse.bacc as bacc
    from concourse.bass_utils import run_bass_kernel_spmd

    def tiles(a):
        a = np.asarray(a).reshape(B // 2, 2, 2, HH, C, L).transpose(0, 2, 3, 1, 4, 5)
        return a.reshape(UNITS, P, L)

    ctx_u = tiles(ctx_2048)
    ctx_g = np.asarray(ctx_2048).reshape(B // 2, 2, 2, HH, C, L).transpose(0, 2, 1, 4, 3, 5)
    up_w = np.concatenate([
        np.concatenate([np.asarray(L0_ffn_W1), np.asarray(L0_ffn_Ws1).reshape(NSH, INTER, L)]),
        np.concatenate([np.asarray(L0_ffn_W3), np.asarray(L0_ffn_Ws3).reshape(NSH, INTER, L)]),
    ], axis=1)
    down_w = np.concatenate([np.asarray(L0_ffn_W2),
                             np.asarray(L0_ffn_Ws2).reshape(L, NSH, INTER).transpose(1, 0, 2)])
    arrays = {
        "x_in": tiles(x),
        "ctx_in": ctx_u,
        "ctxt_in": ctx_u.reshape(UNITS, P, LB, P)[:, :, :, ::-1].transpose(0, 3, 2, 1).reshape(UNITS, P, L),
        "ctxr_in": ctx_g.reshape(UNITS, 2 * C, HH * L),
        "k_in": L0_xattn_k,
        "bias_in": fside_S2_0,
        "wg_in": np.asarray(L0_ffn_Wg).T.reshape(LB, P, E).transpose(1, 0, 2),
        "w13_in": up_w.reshape(E + NSH, 2 * INTER, LB, P).transpose(3, 0, 2, 1),
        "w2_in": down_w.reshape(E + NSH, L, 2, HI).transpose(3, 0, 2, 1),
    }
    arrays = {n: np.ascontiguousarray(a) for n, a in arrays.items()}
    nc = bacc.Bacc("TRN2", target_bir_lowering=False, num_devices=1, dynamic_dma_scratch_size=8192)
    ins = [nc.dram_tensor(n, a.shape, mybir.dt.from_np(a.dtype), kind="ExternalInput").ap() for n, a in arrays.items()]
    out = nc.dram_tensor("out", (UNITS, P, L), F32, kind="ExternalOutput").ap()
    build(nc, *ins, out)
    got = run_bass_kernel_spmd(nc, [arrays], core_ids=[0]).results[0]["out"]
    got = np.asarray(got).reshape(B // 2, 2, HH, 2, C, L).transpose(0, 3, 1, 2, 4, 5)
    return np.ascontiguousarray(got.reshape(B, D, L))
```

```python
from contextlib import ExitStack

import numpy as np

import concourse.bass as bass
from concourse import mybir

ALU = mybir.AluOpType
ACT = mybir.ActivationFunctionType
AX_X = mybir.AxisListType.X
F32 = mybir.dt.float32
BF16 = mybir.dt.bfloat16
I32 = mybir.dt.int32
U32 = mybir.dt.uint32

P = 128
B, D, L = 16, 128, 256
H, C = 16, 8
HH = H // 2
UNITS = B * D // P
LB = L // P
KV = HH * P
EPS = 1e-5

E, TOPK, G = 16, 4, 4
GE = E // G
TOP_G = 2
INTER = 176
HI = INTER // 2
NSH = 2
TOK = B * D
REGION = TOK + P
TILES = TOK * TOPK // P + E
ROW = L + 2 * E
SHARED = NSH * UNITS
STEPS = SHARED + TILES
DEPTH = 4

HEADS = (0, 4, 1, 5)


def build(nc, x_d, ctx_d, ctxt_d, ctxr_d, k_d, bias_d, wg_d, w13_d, w2_d, out_d):
    kpad_d = nc.dram_tensor("kpad_scratch", (H, 3 * P), F32, kind="Internal").ap()
    rows_d = nc.dram_tensor("rows_scratch", ((E + 1) * REGION, ROW), F32, kind="Internal").ap()
    y_d = nc.dram_tensor("y_scratch", (TOPK * TOK + 2 * E * P, L), F32, kind="Internal").ap()

    with ExitStack() as ctx:
        def sb(name, shape, dt=F32):
            return ctx.enter_context(nc.sbuf_tensor(name, shape, dt))

        def sem(name):
            return ctx.enter_context(nc.semaphore(name))

        bank = [ctx.enter_context(nc.psum_tensor(f"bank{i}", [P, 512], F32)) for i in range(8)]

        w13 = sb("w13", [P, E + NSH, LB, 2 * INTER])
        w2 = sb("w2", [HI, E + NSH, 2, L])
        wg = sb("wg", [P, LB, E])
        toep = sb("toep", [P, H, L])
        ctx_rep = sb("ctx_rep", [P, 2, HH, L])
        kv = sb("kv", [P, 2, LB, KV])
        prod = sb("prod", [P, 4, 2, L])
        ctx_n = sb("ctx_n", [P, 2, L])
        ctx_tr = sb("ctx_tr", [P, 2, LB, P])
        v = sb("v", [P, 2, L])
        vc = sb("vc", [P, 2, L])
        v_tr = sb("v_tr", [P, 2, LB, P])
        xn = sb("xn", [P, 2, L])
        xn_tr = sb("xn_tr", [P, 2, LB, P])
        resid = sb("resid", [P, UNITS, L])
        rows = sb("rows", [P, UNITS, ROW])
        xn_tr_all = sb("xn_tr_all", [P, UNITS, LB, P])
        st1 = sb("st1", [P, 2, 16])
        st2 = sb("st2", [P, 2, 16])
        ident = sb("ident", [P, P])
        sum_i = sb("sum_i", [P, 2, 32])
        blocks = sb("blocks", [P, P])
        skip_w = sb("skip_w", [P, 2, P])
        bias_c = sb("bias_c", [P, 2])
        neg_half = sb("neg_half", [P, 1])
        before = sb("before", [P, P], BF16)
        ones = sb("ones", [P, P], BF16)
        low = sb("low", [P, G, G])
        io_e = sb("io_e", [P, E])
        io_tok = sb("io_tok", [P, UNITS, E])
        io_reg = sb("io_reg", [P, E])
        io_j = sb("io_j", [1, E])
        io_t = sb("io_t", [1, TILES])
        pad_row = sb("pad_row", [P, 2, ROW])
        top8 = sb("top8", [P, UNITS, 8])
        top_i = sb("top_i", [P, UNITS, 8], U32)
        sel_bf = sb("sel_bf", [P, UNITS, E], BF16)
        slot_i = sb("slot_i", [P, UNITS, TOPK], I32)
        tile_e = sb("tile_e", [1, TILES], I32)
        tile_row = sb("tile_row", [1, TILES], I32)
        pad_at = sb("pad_at", [1, E], I32)

        skip = vc
        kpad = prod[0:H, :, :, :].rearrange("p g h l -> p (g h l)")[:, 0:3 * P]
        kv_flat = kv[:].rearrange("p q b n -> p (q b n)")
        onehot = kv_flat[:, 0:1024].rearrange("p (t k e) -> p t k e", t=UNITS, k=TOPK)
        wide = kv_flat[:, 1024:2048]
        rt = ctx_rep[:].rearrange("p q h l -> p (q h) l")
        wide_m = kv_flat[0:1, 2048:2048 + TILES * E].rearrange("p (t e) -> p t e", e=E)
        meta = kv_flat[0:1, 2048 + TILES * E:2048 + TILES * (E + 6)].rearrange("p (i t) -> p i t", i=6)
        tf = toep[:].rearrange("p h l -> p (h l)")
        cut = [0]

        def carve(n):
            cut[0] += n
            return tf[:, cut[0] - n:cut[0]]

        xg = [carve(ROW) for _ in range(DEPTH)]
        x_tr = [carve(L).rearrange("p (b n) -> p b n", b=LB) for _ in range(2)]
        act1 = [carve(INTER) for _ in range(2)]
        hid = [carve(INTER) for _ in range(2)]
        hid_tr = [carve(2 * P)[0:HI, :].rearrange("p (b n) -> p b n", b=2) for _ in range(2)]
        y_sb = [carve(L) for _ in range(DEPTH)]
        gate_c = [carve(2) for _ in range(DEPTH)]
        dest_i = [sb(f"dest_i{i}", [P, 1], I32) for i in range(DEPTH)]
        fin = [ctx_rep[:, i, 0:TOPK, :] for i in range(2)]
        fin_a = [kv_flat[:, 2048 * i:2048 * i + L] for i in range(2)]
        fin_b = [kv_flat[:, 2048 * i + L:2048 * i + 2 * L] for i in range(2)]
        fin_o = [kv_flat[:, 2048 * i + 2 * L:2048 * i + 3 * L] for i in range(2)]

        y_ps = [bank[i][:, :].rearrange("p (h l) -> p h l", h=2) for i in range(4)]
        o_ps = bank[4][:, 0:L]
        g_ps = bank[5][:, 0:L]
        tr_ps = bank[6][:, 0:L].rearrange("p (b n) -> p b n", b=LB)
        logit_ps = bank[7][:, 0:UNITS * E]
        rank_ps = bank[6][:, 0:UNITS * E].rearrange("p (t e) -> p t e", e=E)
        count_ps = bank[6][:, 256:256 + UNITS * E].rearrange("p (t e) -> p t e", e=E)
        up_ps = [bank[i][:, 0:2 * INTER] for i in (0, 1)]
        ht_ps = [bank[i][0:HI, 0:2 * P].rearrange("p (b n) -> p b n", b=2) for i in (2, 3)]
        dn_ps = [bank[i][:, 0:L] for i in (4, 5)]
        xt_ps = [bank[i][:, 0:L].rearrange("p (b n) -> p b n", b=LB) for i in (6, 7)]

        wait_taken = sem("wait_taken")
        k_in, k_zero, k_out, toep_in = sem("k_in"), sem("k_zero"), sem("k_out"), sem("toep_in")
        bias_in, wg_in, wsh_in, w_in = sem("bias_in"), sem("wg_in"), sem("wsh_in"), sem("w_in")
        x0_in, x_in = sem("x0_in"), sem("x_in")
        ctr_in, cn_in, cr_in = ([sem(f"{n}{q}") for q in range(2)] for n in ("ctx_tr_in", "ctx_n_in", "ctx_rep_in"))
        const = sem("const")
        skipw_ready = sem("skipw_ready")
        s1a, s1b, s1c, s1d = sem("bn1"), sem("mean1"), sem("vareps1"), sem("rstd1")
        v_ready, vc_ready, vt_ps, vt_ready = sem("v_ready"), sem("vc_ready"), sem("vt_ps"), sem("vt_ready")
        kv0_ready, kv1_ready = sem("kv0_ready"), sem("kv1_ready")
        conv_done, prod_ready, even_done, sum_done = sem("conv_done"), sem("prod_ready"), sem("even_done"), sem("sum_done")
        g_done, skip_ready, xa_ready, resid_ready = sem("g_done"), sem("skip_ready"), sem("xa_ready"), sem("resid_ready")
        s2a, s2b, s2c, s2d, s2e = sem("bn2"), sem("mean2"), sem("vareps2"), sem("rstd2"), sem("shift2")
        xn_ready, row_ready, xt_done, xnt_ready, xnt_all = (
            sem("xn_ready"), sem("row_ready"), sem("xt_done"), sem("xnt_ready"), sem("xnt_all"))
        logits_done = sem("logits_done")
        r = sem("route_step")
        mx_sub, exp_done, sel_ready, rank_done, slots_ready, map_ready = (
            sem("mx_sub"), sem("exp_done"), sem("sel_ready"), sem("rank_done"), sem("slots_ready"), sem("map_ready"))
        scattered, padded = sem("scattered"), sem("padded")
        rows_in = [sem(f"rows_in{b}") for b in range(DEPTH)]
        xtr_ps, xtr_ready, up_done, silu_done, hid_ready, ht_done, htr_ready, dn_done = (
            sem("xtr_ps"), sem("xtr_ready"), sem("up_done"), sem("silu_done"), sem("hid_ready"), sem("ht_done"),
            sem("htr_ready"), sem("dn_done"))
        gate_ready, dest_ready, z_added, y_ready = sem("gate_ready"), sem("dest_ready"), sem("z_added"), sem("y_ready")
        y_sent = [sem(f"y_sent{b}") for b in range(DEPTH)]
        fin_in = [sem("fin_in0"), sem("fin_in1")]
        fa, fb, fc, fo = sem("fin_a"), sem("fin_b"), sem("fin_c"), sem("fin_o")
        out_sent = [sem("out_sent0"), sem("out_sent1")]

        block = ctx.enter_context(nc.Block())

        def v_forward(q):
            part = v[:, q, :]
            return bass.AP(part.tensor, part.offset + P - 1, [list(part.ap[0]), [P, LB], [-1, P]])

        def at_least(eng, s, n):
            if isinstance(n, int) and n <= 0:
                return
            eng.wait_ge(s, n)

        def part(eng):
            eng.sem_inc(wait_taken, 1)

        def units(eng, step):
            step(0, 0, 1, True, False)
            step(1, 1, 2, False, False)
            with eng.Fori(1, UNITS // 2 - 1) as it:
                step(it * 2, 0, it + 1, False, False)
                step(it * 2 + 1, 1, it + 2, False, False)
            step(UNITS - 2, 0, UNITS // 2, False, False)
            step(UNITS - 1, 1, UNITS // 2 + 1, False, True)

        def routed(eng, step):
            for b in range(DEPTH):
                step(b, b, 0)
            with eng.Fori(1, TILES // DEPTH - 1) as it:
                for b in range(DEPTH):
                    step(it * DEPTH + b, b, it)
            for b in range(DEPTH):
                step(TILES - DEPTH + b, b, TILES // DEPTH - 1)

        C_IDENT, C_BLOCKS, C_SUM, C_ALL = 3, 6, 7 + 2 * C, 7 + 2 * C + 11

        @block.sync
        def _(sp):
            def load(u, q):
                late = not (isinstance(u, int) and u < 2)
                if late:
                    sp.wait_ge(kv0_ready, u - 1)
                    sp.wait_ge(kv1_ready, u - 1)
                sp.dma_start(ctx_tr[:, q, :, :].rearrange("p b n -> p (b n)"),
                             ctxt_d[bass.ds(u, 1)].rearrange("a p n -> (a p) n")).then_inc(ctr_in[q], 16)
                if late:
                    sp.wait_ge(skip_ready, u - 1)
                    sp.wait_ge(vc_ready, u - 1)
                sp.dma_start(ctx_n[:, q, :], ctx_d[bass.ds(u, 1)].rearrange("a p l -> (a p) l")).then_inc(cn_in[q], 16)
                if late:
                    sp.wait_ge(prod_ready, (u - 1) * 4)
                src = ctxr_d[bass.ds(u, 1)].rearrange("a g n -> (a g) n")
                src = src.unsqueeze(1).to_broadcast([2 * C, C, HH * L])
                sp.dma_start(ctx_rep[:, q, :, :].rearrange("p h l -> p (h l)"), src).then_inc(cr_in[q], 16)

            def load_expert(e, landed):
                sp.dma_start(w13[:, bass.ds(e, 1), :, :].rearrange("p a b n -> p (a b n)"),
                             w13_d[:, bass.ds(e, 1), :, :].rearrange("p a b n -> p (a b n)")).then_inc(landed, 16)
                sp.dma_start(w2[:, bass.ds(e, 1), :, :].rearrange("p a b n -> p (a b n)"),
                             w2_d[:, bass.ds(e, 1), :, :].rearrange("p a b n -> p (a b n)")).then_inc(landed, 16)

            sp.dma_start(resid[:, 0, :], x_d[0]).then_inc(x0_in, 16)
            sp.wait_ge(k_zero, 1)
            sp.dma_start(kpad[:, P - 1:P - 1 + L], k_d).then_inc(k_in, 16)
            for q in range(2):
                for hh in range(HH):
                    head = bias_d[(q * HH + hh) * C:(q * HH + hh + 1) * C]
                    sp.dma_start(bias_c[hh * 2 * C:(hh + 1) * 2 * C, q:q + 1],
                                 bass.AP(head.tensor, head.offset, [[0, 2], [1, C], [1, 1]])).then_inc(bias_in, 16)
            sp.wait_ge(k_in, 16)
            sp.dma_start(kpad_d, kpad).then_inc(k_out, 16)
            load(0, 0)
            sp.wait_ge(k_out, 16)
            first = kpad_d[0:H, 0:L]
            window = bass.AP(first.tensor, first.offset, [[1, P], [3 * P, H], [1, L]])
            sp.dma_start(toep[:], window).then_inc(toep_in, 16)
            sp.dma_start(resid[:, 1:, :], x_d[1:].rearrange("u p l -> p u l")).then_inc(x_in, 16)
            load(1, 1)
            sp.dma_start(wg[:], wg_d).then_inc(wg_in, 16)
            for i in range(NSH):
                load_expert(E + i, wsh_in)
                load_expert(i, w_in)
            with sp.Fori(1, UNITS // 2) as it:
                load(it * 2, 0)
                load_expert(it * 2, w_in)
                load(it * 2 + 1, 1)
                load_expert(it * 2 + 1, w_in)
            sp.wait_ge(map_ready, 1)
            with sp.Fori(0, E) as e:
                at = sp.value_load(pad_at[0:1, bass.ds(e, 1)], min_val=0, max_val=E * REGION)
                sp.dma_start(rows_d[bass.ds(at, P)], pad_row[:, 0, :]).then_inc(padded, 16)
            sp.dma_start(rows_d[E * REGION:E * REGION + P], pad_row[:, 1, :]).then_inc(padded, 16)
            sp.wait_ge(padded, 16 * (E + 1))
            sp.wait_ge(scattered, 16 * UNITS * TOPK)

            def gather(t, b, before):
                if not (isinstance(t, int) and t < DEPTH):
                    sp.wait_ge(xtr_ps, t - (DEPTH - 1))
                    sp.wait_ge(dest_ready, t - (DEPTH - 1))
                at = sp.value_load(tile_row[0:1, bass.ds(t, 1)], min_val=0, max_val=E * REGION)
                sp.dma_start(xg[b], rows_d[bass.ds(at, P)]).then_inc(rows_in[b], 16)

            routed(sp, gather)
            for b in range(DEPTH):
                sp.wait_ge(y_sent[b], 16 * (TILES // DEPTH))
            y_v = y_d[0:TOPK * TOK].rearrange("(k n) l -> n k l", k=TOPK)

            def final(u, q, first=False):
                if not first:
                    sp.wait_ge(fa, u - 1)
                    sp.wait_ge(fb, u - 1)
                sp.dma_start(fin[q], y_v[bass.ds(u * P, P)]).then_inc(fin_in[q], 16)

            def store(u, q):
                sp.wait_ge(fo, u + 1)
                sp.dma_start(out_d[bass.ds(u, 1)].rearrange("a p l -> (a p) l"), fin_o[q]).then_inc(out_sent[q], 16)

            final(0, 0, True)
            final(1, 1, True)
            with sp.Fori(1, UNITS // 2) as it:
                final(it * 2, 0)
                store(it * 2 - 2, 0)
                final(it * 2 + 1, 1)
                store(it * 2 - 1, 1)
            store(UNITS - 2, 0)
            store(UNITS - 1, 1)
            sp.wait_ge(out_sent[0], 16 * (UNITS // 2))
            sp.wait_ge(out_sent[1], 16 * (UNITS // 2))

        @block.scalar
        def _(act):
            def copy_v(u, q):
                act.wait_ge(vt_ps, u + 1)
                if not (isinstance(u, int) and u < 2):
                    act.wait_ge(kv0_ready, u - 1)
                    act.wait_ge(kv1_ready, u - 1)
                nc.scalar.activation(v_tr[:, q, :, :], tr_ps, ACT.Copy).then_inc(vt_ready, 1)

            def normal(u, q):
                act.wait_ge(s2e, u + 1)
                if not (isinstance(u, int) and u < 2):
                    act.wait_ge(xt_done, u - 1)
                part(act)
                nc.scalar.activation(xn[:, q, :], resid[:, bass.ds(u, 1), :].rearrange("p a l -> p (a l)"),
                                     ACT.Identity, bias=st2[:, q, 10:11], scale=st2[:, q, 9:10]).then_inc(xn_ready, 1)
                nc.scalar.activation(rows[:, bass.ds(u, 1), 0:L].rearrange("p a l -> p (a l)"),
                                     resid[:, bass.ds(u, 1), :].rearrange("p a l -> p (a l)"),
                                     ACT.Identity, bias=st2[:, q, 10:11], scale=st2[:, q, 9:10]).then_inc(row_ready, 1)

            def copy_xn(u, q):
                act.wait_ge(xt_done, u + 1)
                if not (isinstance(u, int) and u < 2):
                    act.wait_ge(logits_done, u - 1)
                nc.scalar.activation(xn_tr[:, q, :, :], tr_ps, ACT.Copy).then_inc(xnt_ready, 1)
                nc.scalar.activation(xn_tr_all[:, bass.ds(u, 1), :, :].rearrange("p a b n -> p (a b) n"), tr_ps,
                                     ACT.Copy).then_inc(xnt_all, 1)

            def step(u, q, landed, first, last):
                if not last:
                    copy_v(u + 1, 1 - q)
                if not first:
                    normal(u - 1, 1 - q)
                    copy_xn(u - 1, 1 - q)

            copy_v(0, 0)
            units(act, step)
            normal(UNITS - 1, 1)
            copy_xn(UNITS - 1, 1)

            act.wait_ge(mx_sub, 1)
            nc.scalar.activation(rt[:, 1, :], rt[:, 0, :], ACT.Exp).then_inc(exp_done, 1)
            nc.scalar.preload_act_table(ACT.Silu)

            def src_tr(w, p, tile=None):
                if not (isinstance(w, int) and w < 2):
                    act.wait_ge(up_done, w - 1)
                if tile is None:
                    act.wait_ge(xtr_ps, w - SHARED + 1)
                    src = xt_ps[p]
                else:
                    src = xn_tr_all[:, bass.ds(tile, 1), :, :].rearrange("p a b n -> p (a b) n")
                part(act)
                nc.scalar.activation(x_tr[p], src, ACT.Copy).then_inc(xtr_ready, 1)

            def silu(w, p):
                act.wait_ge(up_done, w + 1)
                if not (isinstance(w, int) and w < 2):
                    act.wait_ge(hid_ready, w - 1)
                nc.scalar.activation(act1[p], up_ps[p][:, 0:INTER], ACT.Silu).then_inc(silu_done, 1)

            def store_y(t, p, b, before):
                act.wait_ge(dn_done, t + (SHARED + 1))
                at_least(act, y_sent[b], before * 16)
                nc.scalar.activation(y_sb[b], dn_ps[p], ACT.Copy).then_inc(y_ready, 1)

            act.wait_ge(xnt_all, UNITS)
            act.wait_ge(conv_done, 4 * UNITS)
            src_tr(0, 0, 0)
            silu(0, 0)
            src_tr(1, 1, 0)
            with act.Fori(1, UNITS) as it:
                silu(it * 2 - 1, 1)
                src_tr(it * 2, 0, it)
                silu(it * 2, 0)
                src_tr(it * 2 + 1, 1, it)
            silu(SHARED - 1, 1)
            src_tr(SHARED, 0)

            def routed_step(t, b, before):
                p = b % 2
                silu(t + SHARED, p)
                if not (isinstance(t, int) and t == TILES - 1):
                    src_tr(t + (SHARED + 1), 1 - p)
                if not (isinstance(t, int) and t < 2):
                    store_y(t - 2, p, (b - 2) % DEPTH, before if b >= 2 else before - 1)

            routed(act, routed_step)
            store_y(TILES - 2, 0, DEPTH - 2, TILES // DEPTH - 1)
            store_y(TILES - 1, 1, DEPTH - 1, TILES // DEPTH - 1)

        @block.gpsimd
        def _(pool):
            n = [0]

            def done(ins):
                n[0] += 1
                ins.then_inc(const, 1)
                pool.wait_ge(const, n[0])

            nc.gpsimd.memset(kpad, 0.0).then_inc(k_zero, 1)
            done(nc.gpsimd.memset(neg_half[:], -0.5))
            done(nc.gpsimd.memset(ident[:], 0.0))
            done(nc.gpsimd.affine_select(out=ident[:], in_=ident[:], compare_op=ALU.not_equal, fill=1.0, base=0,
                                         pattern=[[-1, P]], channel_multiplier=1))
            done(nc.gpsimd.memset(blocks[:], 1.0))
            bv = blocks[:].rearrange("p (n j) -> p n j", j=C)
            done(nc.gpsimd.affine_select(out=bv, in_=bv, compare_op=ALU.is_ge, fill=0.0, base=0,
                                         pattern=[[-C, P // C], [0, C]], channel_multiplier=1))
            done(nc.gpsimd.affine_select(out=bv, in_=bv, compare_op=ALU.is_ge, fill=0.0, base=C - 1,
                                         pattern=[[C, P // C], [0, C]], channel_multiplier=-1))
            done(nc.gpsimd.memset(sum_i[:], 0.0))

            def v_stats(u, q):
                pool.wait_ge(s1b, u + 1)
                part(pool)
                nc.gpsimd.tensor_scalar(st1[:, q, 8:9], st1[:, q, 7:8], EPS, None, ALU.add).then_inc(s1c, 1)
                pool.wait_ge(s1c, u + 1)
                nc.gpsimd.tensor_tensor(st1[:, q, 9:10], st1[:, q, 8:9], neg_half[:], ALU.pow).then_inc(s1d, 1)

            v_stats(0, 0)
            for i in range(C):
                for par in range(2):
                    sv = sum_i[:, par, 16 * par:16 * par + 16].rearrange("p (b j) -> p b j", j=C)
                    done(nc.gpsimd.affine_select(out=sv, in_=sv, compare_op=ALU.not_equal, fill=1.0, base=-C * i,
                                                 pattern=[[-64, 2], [-1, C]], channel_multiplier=1))
            assert n[0] == 7 + 2 * C

            def v_work(u, q, landed):
                pool.wait_ge(v_ready, u + 1)
                if not (isinstance(u, int) and u < 2):
                    pool.wait_ge(resid_ready, u - 1)
                pool.wait_ge(cn_in[q], landed * 16)
                nc.gpsimd.tensor_tensor(vc[:, q, :].rearrange("p (b n) -> p b n", b=LB), v_forward(q),
                                        ctx_n[:, q, :].rearrange("p (b n) -> p b n", b=LB), ALU.mult).then_inc(vc_ready, 1)
                pool.wait_ge(vt_ready, u + 1)
                if not (isinstance(u, int) and u < 2):
                    pool.wait_ge(conv_done, 4 * (u - 1))
                pool.wait_ge(ctr_in[q], landed * 16)
                nc.gpsimd.tensor_tensor(
                    kv[:, q, 1, :].rearrange("p (g i j) -> p g i j", i=C, j=C),
                    v_tr[:, q, 1, :].rearrange("p (g i) -> p g i", i=C).unsqueeze(3).to_broadcast([P, 2 * HH, C, C]),
                    ctx_tr[:, q, 1, :].rearrange("p (g j) -> p g j", j=C).unsqueeze(2).to_broadcast([P, 2 * HH, C, C]),
                    ALU.mult).then_inc(kv1_ready, 1)

            def x_work(u, q):
                pool.wait_ge(xa_ready, u + 1)
                pool.wait_ge(skip_ready, u + 1)
                rv = resid[:, bass.ds(u, 1), :].rearrange("p a l -> p (a l)")
                nc.gpsimd.tensor_tensor(rv, rv, skip[:, q, :], ALU.add).then_inc(resid_ready, 1)
                pool.wait_ge(s2b, u + 1)
                part(pool)
                nc.gpsimd.tensor_scalar(st2[:, q, 8:9], st2[:, q, 7:8], EPS, None, ALU.add).then_inc(s2c, 1)
                pool.wait_ge(s2c, u + 1)
                nc.gpsimd.tensor_tensor(st2[:, q, 9:10], st2[:, q, 8:9], neg_half[:], ALU.pow).then_inc(s2d, 1)

            def step(u, q, landed, first, last):
                if not last:
                    v_stats(u + 1, 1 - q)
                if not first:
                    x_work(u - 1, 1 - q)
                if not last:
                    v_work(u + 1, 1 - q, landed)

            v_work(0, 0, 1)
            units(pool, step)
            x_work(UNITS - 1, 1)

            done(nc.gpsimd.memset(ones[:], 1.0))
            done(nc.gpsimd.affine_select(out=before[:], in_=ones[:], compare_op=ALU.is_gt, fill=0.0, base=0,
                                         pattern=[[1, P]], channel_multiplier=-1))
            done(nc.gpsimd.memset(low[:], 1.0))
            done(nc.gpsimd.affine_select(out=low[:], in_=low[:], compare_op=ALU.is_gt, fill=0.0, base=0,
                                         pattern=[[1, G], [-1, G]], channel_multiplier=0))
            exact = dict(allow_small_or_imprecise_dtypes=True)
            done(nc.gpsimd.iota(io_e[:], [[1, E]], base=0, channel_multiplier=0, **exact))
            done(nc.gpsimd.iota(io_tok[:], [[P, UNITS], [0, E]], base=0, channel_multiplier=1, **exact))
            done(nc.gpsimd.iota(io_reg[:], [[REGION, E]], base=0, channel_multiplier=0, **exact))
            done(nc.gpsimd.iota(io_j[:], [[P, E]], base=0, channel_multiplier=0, **exact))
            done(nc.gpsimd.iota(io_t[:], [[1, TILES]], base=0, channel_multiplier=0, **exact))
            done(nc.gpsimd.memset(pad_row[:, :, 0:L + E], 0.0))
            done(nc.gpsimd.iota(pad_row[:, :, L + E:], [[E * P, 2], [P, E]], base=TOPK * TOK, channel_multiplier=1,
                                **exact))

            pool.wait_ge(row_ready, UNITS)
            pool.wait_ge(slots_ready, 1)
            for u in range(UNITS):
                for k in range(TOPK):
                    pool.indirect_dma_start(
                        rows_d, bass.IndirectOffsetOnAxis(ap=slot_i[:, u, k:k + 1].bitcast(U32), axis=0),
                        rows[:, u, :], None).then_inc(scattered, 16)

            def send(t, b):
                pool.wait_ge(y_ready, t + 1)
                pool.wait_ge(dest_ready, t + 1)
                part(pool)
                pool.indirect_dma_start(
                    y_d, bass.IndirectOffsetOnAxis(ap=dest_i[b][:, 0:1].bitcast(U32), axis=0),
                    y_sb[b], None).then_inc(y_sent[b], 16)

            with pool.Fori(0, TILES // DEPTH) as it:
                for b in range(DEPTH):
                    send(it * DEPTH + b, b)

            def final(u, q, landed):
                pool.wait_ge(fin_in[q], landed * 16)
                if not (isinstance(u, int) and u < 2):
                    pool.wait_ge(fo, u - 1)
                nc.gpsimd.tensor_tensor(fin_b[q], fin[q][:, 3, :],
                                        resid[:, bass.ds(u, 1), :].rearrange("p a l -> p (a l)"),
                                        ALU.add).then_inc(fb, 1)

            pool.wait_ge(z_added, UNITS)
            final(0, 0, 1)
            final(1, 1, 1)
            with pool.Fori(1, UNITS // 2) as it:
                final(it * 2, 0, it + 1)
                final(it * 2 + 1, 1, it + 1)

        @block.vector
        def _(dve):
            def tile(u):
                return resid[:, bass.ds(u, 1), :].rearrange("p a l -> p (a l)")

            def stats1(u, q):
                if isinstance(u, int) and u == 0:
                    dve.wait_ge(x0_in, 16)
                else:
                    dve.wait_ge(x_in, 16)
                nc.vector.bn_stats(st1[:, q, 0:6], tile(u)).then_inc(s1a, 1)
                dve.wait_ge(s1a, u + 1)
                part(dve)
                nc.vector.bn_aggr(st1[:, q, 6:8], st1[:, q, 0:6]).then_inc(s1b, 1)

            def norm1(u, q):
                dve.wait_ge(s1d, u + 1)
                if not (isinstance(u, int) and u < 2):
                    dve.wait_ge(vt_ps, u - 1)
                    dve.wait_ge(vc_ready, u - 1)
                nc.vector.tensor_scalar(v_forward(q), tile(u).rearrange("p (b n) -> p b n", b=LB), st1[:, q, 6:7], st1[:, q, 9:10],
                                        ALU.subtract, ALU.mult).then_inc(v_ready, 1)

            def kv_block0(u, q, landed):
                dve.wait_ge(ctr_in[q], landed * 16)
                dve.wait_ge(vt_ready, u + 1)
                if not (isinstance(u, int) and u < 2):
                    dve.wait_ge(conv_done, 4 * (u - 1))
                nc.vector.tensor_tensor(
                    kv[:, q, 0, :].rearrange("p (g i j) -> p g i j", i=C, j=C),
                    v_tr[:, q, 0, :].rearrange("p (g i) -> p g i", i=C).unsqueeze(3).to_broadcast([P, 2 * HH, C, C]),
                    ctx_tr[:, q, 0, :].rearrange("p (g j) -> p g j", j=C).unsqueeze(2).to_broadcast([P, 2 * HH, C, C]),
                    ALU.mult).then_inc(kv0_ready, 1)

            def product(u, q, g, landed, first):
                dve.wait_ge(conv_done, 4 * u + g + 1)
                if g == 0:
                    dve.wait_ge(cr_in[q], (landed - q) * 16)
                if not first:
                    dve.wait_ge(even_done if g < 2 else sum_done, u)
                h0 = HEADS[g]
                nc.vector.tensor_tensor(prod[:, g, :, :], y_ps[g], ctx_rep[:, q, h0:h0 + 3:2, :],
                                        ALU.mult).then_inc(prod_ready, 1)

            def add_x(u, q):
                dve.wait_ge(sum_done, u + 1)
                nc.vector.tensor_tensor(tile(u), o_ps, tile(u), ALU.add).then_inc(xa_ready, 1)

            def skip_term(u, q):
                dve.wait_ge(g_done, u + 1)
                if not (isinstance(u, int) and u < 2):
                    dve.wait_ge(resid_ready, u - 1)
                nc.vector.tensor_tensor(skip[:, q, :], g_ps, ctx_n[:, q, :], ALU.mult).then_inc(skip_ready, 1)

            def stats2(u, q):
                dve.wait_ge(resid_ready, u + 1)
                part(dve)
                nc.vector.bn_stats(st2[:, q, 0:6], tile(u)).then_inc(s2a, 1)
                dve.wait_ge(s2a, u + 1)
                if not (isinstance(u, int) and u < 2):
                    dve.wait_ge(row_ready, u - 1)
                part(dve)
                nc.vector.bn_aggr(st2[:, q, 6:8], st2[:, q, 0:6]).then_inc(s2b, 1)

            def shift2(u, q):
                dve.wait_ge(s2d, u + 1)
                nc.vector.scalar_tensor_tensor(st2[:, q, 10:11], st2[:, q, 6:7], -1.0, st2[:, q, 9:10],
                                               ALU.mult, ALU.mult).then_inc(s2e, 1)

            def step(u, q, landed, first, last):
                if not last:
                    stats1(u + 1, 1 - q)
                product(u, q, 0, landed, first)
                if not last:
                    norm1(u + 1, 1 - q)
                if not first:
                    add_x(u - 1, 1 - q)
                product(u, q, 1, landed, first)
                skip_term(u, q)
                if not first:
                    stats2(u - 1, 1 - q)
                product(u, q, 2, landed, first)
                if not first:
                    shift2(u - 1, 1 - q)
                if not last:
                    kv_block0(u + 1, 1 - q, landed)
                product(u, q, 3, landed, first)

            stats1(0, 0)
            norm1(0, 0)
            kv_block0(0, 0, 1)
            dve.wait_ge(bias_in, 16 * 2 * HH)
            dve.wait_ge(const, C_BLOCKS)
            for q in range(2):
                nc.vector.tensor_scalar(skip_w[:, q, :], blocks[:], bias_c[:, q:q + 1], None, ALU.mult
                                        ).then_inc(skipw_ready, 1)
            units(dve, step)
            add_x(UNITS - 1, 1)
            stats2(UNITS - 1, 1)
            shift2(UNITS - 1, 1)

            n = [0]

            def then(ins):
                n[0] += 1
                ins.then_inc(r, 1)
                dve.wait_ge(r, n[0])

            te = lambda i: rt[:, i, :].rearrange("p (t e) -> p t e", e=E)
            lg = logit_ps.rearrange("p (t e) -> p t e", e=E)
            mx = rt[:, 2, 0:UNITS]
            dve.wait_ge(logits_done, UNITS)
            then(nc.vector.tensor_reduce(mx, lg, AX_X, ALU.max))
            nc.vector.tensor_tensor(te(0), lg, mx.unsqueeze(2).to_broadcast([P, UNITS, E]),
                                    ALU.subtract).then_inc(mx_sub, 1)
            dve.wait_ge(exp_done, 1)
            then(nc.vector.tensor_reduce(rt[:, 2, 16:32], te(1), AX_X, ALU.add))
            then(nc.vector.reciprocal(rt[:, 2, 32:48], rt[:, 2, 16:32]))
            then(nc.vector.tensor_tensor(te(3), te(1), rt[:, 2, 32:48].unsqueeze(2).to_broadcast([P, UNITS, E]),
                                         ALU.mult))
            gm = rt[:, 2, 64:64 + UNITS * G].rearrange("p (t g) -> p t g", g=G)
            then(nc.vector.tensor_reduce(rt[:, 2, 64:64 + UNITS * G], rt[:, 3, :].rearrange("p (n i) -> p n i", i=GE),
                                         AX_X, ALU.max))
            other = gm.unsqueeze(2).to_broadcast([P, UNITS, G, G])
            own = gm.unsqueeze(3).to_broadcast([P, UNITS, G, G])
            tgg = lambda i: rt[:, i, :].rearrange("p (t g o) -> p t g o", g=G, o=G)
            then(nc.vector.tensor_tensor(tgg(4), other, own, ALU.is_equal))
            then(nc.vector.tensor_tensor(tgg(5), other, own, ALU.is_gt))
            dve.wait_ge(const, C_ALL)
            then(nc.vector.tensor_tensor(tgg(4), tgg(4), low[:].unsqueeze(1).to_broadcast([P, UNITS, G, G]), ALU.mult))
            then(nc.vector.tensor_tensor(tgg(5), tgg(4), tgg(5), ALU.add))
            then(nc.vector.tensor_reduce(rt[:, 2, 128:192], rt[:, 5, :].rearrange("p (n o) -> p n o", o=G),
                                         AX_X, ALU.add))
            then(nc.vector.tensor_scalar(rt[:, 2, 192:256], rt[:, 2, 128:192], TOP_G - 0.5, None, ALU.is_lt))
            kept = rt[:, 2, 192:256].unsqueeze(2).to_broadcast([P, UNITS * G, GE])
            ng = lambda i: rt[:, i, :].rearrange("p (n i) -> p n i", i=GE)
            then(nc.vector.tensor_tensor(ng(4), ng(3), kept, ALU.mult))
            then(nc.vector.scalar_tensor_tensor(ng(5), kept, -1.0, ng(4), ALU.add, ALU.add))
            for t in range(UNITS):
                last = nc.vector.max(top8[:, t, :], te(5)[:, t, :])
            then(last)
            for t in range(UNITS):
                last = nc.vector.max_index(top_i[:, t, :], top8[:, t, :], te(5)[:, t, :])
            then(last)
            idx_f = rt[:, 6, 0:UNITS * TOPK].rearrange("p (t k) -> p t k", k=TOPK)
            then(nc.vector.tensor_copy(idx_f, top_i[:, :, 0:TOPK]))
            then(nc.vector.tensor_tensor(onehot, idx_f.unsqueeze(3).to_broadcast([P, UNITS, TOPK, E]),
                                         io_e[:].unsqueeze(1).unsqueeze(1).to_broadcast([P, UNITS, TOPK, E]),
                                         ALU.is_equal))
            then(nc.vector.tensor_tensor(te(4), onehot[:, :, 0, :], onehot[:, :, 1, :], ALU.add))
            then(nc.vector.tensor_tensor(te(6), onehot[:, :, 2, :], onehot[:, :, 3, :], ALU.add))
            then(nc.vector.tensor_tensor(te(7), te(4), te(6), ALU.add))
            nc.vector.tensor_copy(sel_bf[:], te(7)).then_inc(sel_ready, 1)
            then(nc.vector.tensor_tensor(rows[:, :, L:L + E], te(7), te(3), ALU.mult))
            then(nc.vector.scalar_tensor_tensor(te(8), onehot[:, :, 2, :], 2.0, onehot[:, :, 1, :], ALU.mult, ALU.add))
            then(nc.vector.scalar_tensor_tensor(te(9), onehot[:, :, 3, :], 3.0, te(8), ALU.mult, ALU.add))
            then(nc.vector.scalar_tensor_tensor(rows[:, :, L + E:], te(9), float(TOK), io_tok[:], ALU.mult, ALU.add))
            dve.wait_ge(rank_done, 1)
            then(nc.vector.tensor_tensor(te(8), rank_ps, io_reg[:].unsqueeze(1).to_broadcast([P, UNITS, E]), ALU.add))
            wv = wide.rearrange("p (t k e) -> p t k e", k=TOPK, e=E)
            then(nc.vector.tensor_tensor(wv, onehot, te(8).unsqueeze(2).to_broadcast([P, UNITS, TOPK, E]), ALU.mult))
            then(nc.vector.tensor_reduce(rt[:, 6, 64:128], wide.rearrange("p (n e) -> p n e", e=E), AX_X, ALU.add))
            nc.vector.tensor_copy(slot_i[:].rearrange("p t k -> p (t k)"), rt[:, 6, 64:128]).then_inc(slots_ready, 1)
            cnt, tiles_e = meta[:, 0, 0:E], meta[:, 0, E:2 * E]
            then(nc.vector.tensor_reduce(cnt, count_ps[0:1].rearrange("p t e -> p e t"), AX_X, ALU.add))
            jj = wide_m[:, 0:E, :]
            then(nc.vector.tensor_tensor(jj, cnt.unsqueeze(2).to_broadcast([1, E, E]),
                                         io_j[:].unsqueeze(1).to_broadcast([1, E, E]), ALU.is_gt))
            then(nc.vector.tensor_reduce(tiles_e, jj, AX_X, ALU.add))
            upto = [meta[:, 1, 0:E], meta[:, 1, E:2 * E]]
            then(nc.vector.tensor_copy(upto[0], tiles_e))
            for i, sh in enumerate((1, 2, 4, 8)):
                a, b = upto[i % 2], upto[1 - i % 2]
                then(nc.vector.tensor_copy(b[:, 0:sh], a[:, 0:sh]))
                then(nc.vector.tensor_tensor(b[:, sh:], a[:, sh:], a[:, 0:E - sh], ALU.add))
            then(nc.vector.tensor_tensor(wide_m, io_t[:].unsqueeze(2).to_broadcast([1, TILES, E]),
                                         upto[0].unsqueeze(1).to_broadcast([1, TILES, E]), ALU.is_ge))
            then(nc.vector.tensor_reduce(meta[:, 2, :], wide_m, AX_X, ALU.add))
            then(nc.vector.tensor_tensor(wide_m, wide_m, tiles_e.unsqueeze(1).to_broadcast([1, TILES, E]), ALU.mult))
            then(nc.vector.tensor_reduce(meta[:, 3, :], wide_m, AX_X, ALU.add))
            then(nc.vector.tensor_tensor(meta[:, 4, :], io_t[:], meta[:, 3, :], ALU.subtract))
            then(nc.vector.tensor_scalar(meta[:, 5, :], meta[:, 2, :], float(REGION), None, ALU.mult))
            then(nc.vector.scalar_tensor_tensor(meta[:, 3, :], meta[:, 4, :], float(P), meta[:, 5, :],
                                                ALU.mult, ALU.add))
            then(nc.vector.tensor_scalar(tile_row[:], meta[:, 3, :], float(E * REGION), None, ALU.min))
            then(nc.vector.tensor_scalar(meta[:, 5, :], meta[:, 2, :], E - 0.5, None, ALU.is_gt))
            then(nc.vector.scalar_tensor_tensor(meta[:, 3, :], meta[:, 4, :], float(-E), meta[:, 5, :],
                                                ALU.add, ALU.mult))
            then(nc.vector.tensor_tensor(tile_e[:], meta[:, 3, :], meta[:, 2, :], ALU.add))
            nc.vector.tensor_tensor(pad_at[:], cnt, io_reg[0:1, :], ALU.add).then_inc(map_ready, 1)

            def hidden(w, p, t=None, b=0):
                dve.wait_ge(silu_done, w + 1)
                if not (isinstance(w, int) and w < 2):
                    dve.wait_ge(ht_done, w - 1)
                if t is None:
                    nc.vector.tensor_tensor(hid[p], act1[p], up_ps[p][:, INTER:], ALU.mult).then_inc(hid_ready, 1)
                else:
                    dve.wait_ge(gate_ready, t + 1)
                    nc.vector.scalar_tensor_tensor(hid[p], act1[p], gate_c[b][:, 0:1], up_ps[p][:, INTER:],
                                                   ALU.mult, ALU.mult).then_inc(hid_ready, 1)

            def copy_h(w, p):
                dve.wait_ge(ht_done, w + 1)
                if not (isinstance(w, int) and w < 2):
                    dve.wait_ge(dn_done, w - 1)
                nc.vector.tensor_copy(hid_tr[p], ht_ps[p]).then_inc(htr_ready, 1)

            def add_z(t):
                dve.wait_ge(dn_done, t * 2 + 2)
                rv = resid[:, bass.ds(t, 1), :].rearrange("p a l -> p (a l)")
                nc.vector.tensor_tensor(rv, dn_ps[0], rv, ALU.add).then_inc(z_added, 1)

            def take(t, b, before):
                dve.wait_ge(rows_in[b], before * 16 + 16)
                if not (isinstance(t, int) and t < DEPTH):
                    dve.wait_ge(hid_ready, t + (SHARED + 1 - DEPTH))
                    dve.wait_ge(y_sent[b], before * 16)
                e = dve.value_load(tile_e[0:1, bass.ds(t, 1)], min_val=0, max_val=E - 1)
                nc.vector.tensor_copy(gate_c[b][:, 0:1], xg[b][:, bass.ds(e + L, 1)]).then_inc(gate_ready, 1)
                nc.vector.tensor_copy(dest_i[b][:, 0:1], xg[b][:, bass.ds(e + (L + E), 1)]).then_inc(dest_ready, 1)

            hidden(0, 0)
            copy_h(0, 0)
            hidden(1, 1)
            with dve.Fori(1, UNITS) as it:
                copy_h(it * 2 - 1, 1)
                hidden(it * 2, 0)
                copy_h(it * 2, 0)
                hidden(it * 2 + 1, 1)
                add_z(it - 1)

            def routed_step(t, b, before):
                take(t, b, before)
                copy_h(t + (SHARED - 1), 1 - b % 2)
                hidden(t + SHARED, b % 2, t, b)
                if isinstance(t, int) and t == 1:
                    add_z(UNITS - 1)

            routed(dve, routed_step)
            copy_h(STEPS - 1, 1)

            def final(u, q, pair):
                dve.wait_ge(fin_in[q], pair * 16 + 16)
                nc.vector.tensor_tensor(fin_a[q], fin[q][:, 0, :], fin[q][:, 1, :], ALU.add).then_inc(fc, 1)
                dve.wait_ge(fc, u + 1)
                nc.vector.tensor_tensor(fin_a[q], fin_a[q], fin[q][:, 2, :], ALU.add).then_inc(fa, 1)
                dve.wait_ge(fa, u + 1)
                dve.wait_ge(fb, u + 1)
                at_least(dve, out_sent[q], pair * 16)
                nc.vector.tensor_tensor(fin_o[q], fin_a[q], fin_b[q], ALU.add).then_inc(fo, 1)

            final(0, 0, 0)
            final(1, 1, 0)
            with dve.Fori(1, UNITS // 2) as it:
                final(it * 2, 0, it)
                final(it * 2 + 1, 1, it)

        @block.tensor
        def _(pe):
            def transpose_v(u, q):
                pe.wait_ge(v_ready, u + 1)
                if not (isinstance(u, int) and u < 3):
                    pe.wait_ge(xnt_all, u - 2)
                for blk in range(LB):
                    last = nc.tensor.transpose(tr_ps[:, blk, :], v[:, q, blk * P:(blk + 1) * P], ident[:])
                last.then_inc(vt_ps, 1)

            def convolve(u, q, g):
                if g == 0:
                    pe.wait_ge(kv0_ready, u + 1)
                    pe.wait_ge(kv1_ready, u + 1)
                if not (isinstance(u, int) and u < 1):
                    pe.wait_ge(prod_ready, u * 4 + (g - 3))
                for s in range(2):
                    h = HEADS[g] + 2 * s
                    nc.tensor.matmul(y_ps[g][:, s, :], kv[:, q, 0, h * P:(h + 1) * P], toep[:, q * HH + h, :],
                                     start=True, stop=False)
                    last = nc.tensor.matmul(y_ps[g][:, s, P:], kv[:, q, 1, h * P:(h + 1) * P],
                                            toep[:, q * HH + h, 0:P], start=False, stop=True)
                last.then_inc(conv_done, 1)

            def sums(u, par):
                pe.wait_ge(prod_ready, u * 4 + 2 + 2 * par)
                if par == 0 and not (isinstance(u, int) and u < 1):
                    pe.wait_ge(xa_ready, u)
                for c in range(4):
                    last = nc.tensor.matmul(bank[4][32 * c:32 * c + 32, 0:L], sum_i[:, par, :],
                                            prod[:, 2 * par + c // 2, c % 2, :], start=par == 0, stop=par == 1)
                last.then_inc(sum_done if par else even_done, 1)

            def skip_sum(u, q):
                pe.wait_ge(vc_ready, u + 1)
                if not (isinstance(u, int) and u < 1):
                    pe.wait_ge(skip_ready, u)
                nc.tensor.matmul(g_ps, skip_w[:, q, :], vc[:, q, :], start=True, stop=True).then_inc(g_done, 1)

            def router(u, q):
                pe.wait_ge(xn_ready, u + 1)
                if isinstance(u, int) and u + 3 > UNITS:
                    pe.wait_ge(vt_ready, UNITS)
                    at_least(pe, xnt_all, u)
                else:
                    pe.wait_ge(vt_ready, u + 3)
                for blk in range(LB):
                    last = nc.tensor.transpose(tr_ps[:, blk, :], xn[:, q, blk * P:(blk + 1) * P], ident[:])
                last.then_inc(xt_done, 1)
                pe.wait_ge(xnt_ready, u + 1)
                for blk in range(LB):
                    last = nc.tensor.matmul(logit_ps[:, bass.ds(u * E, E)], xn_tr[:, q, blk, :], wg[:, blk, :],
                                            start=blk == 0, stop=blk == LB - 1)
                last.then_inc(logits_done, 1)

            def step(u, q, landed, first, last):
                convolve(u, q, 0)
                if not first:
                    sums(u - 1, 1)
                convolve(u, q, 1)
                skip_sum(u, q)
                if not last:
                    transpose_v(u + 1, 1 - q)
                convolve(u, q, 2)
                sums(u, 0)
                convolve(u, q, 3)
                if not first:
                    router(u - 1, 1 - q)

            pe.wait_ge(const, C_SUM)
            transpose_v(0, 0)
            pe.wait_ge(toep_in, 16)
            pe.wait_ge(skipw_ready, 2)
            pe.wait_ge(wg_in, 16)
            units(pe, step)
            sums(UNITS - 1, 1)
            router(UNITS - 1, 1)

            pe.wait_ge(sel_ready, 1)
            pe.wait_ge(xnt_all, UNITS)
            nc.tensor.matmul(count_ps, ones[:], sel_bf[:], start=True, stop=True)
            nc.tensor.matmul(rank_ps, before[:], sel_bf[:], start=True, stop=False)
            for t in range(UNITS - 1):
                last = nc.tensor.matmul(rank_ps[:, t + 1:, :], ones[:],
                                        sel_bf[:, t:t + 1, :].to_broadcast([P, UNITS - 1 - t, E]),
                                        start=False, stop=t == UNITS - 2)
            last.then_inc(rank_done, 1)

            def expert(t):
                return pe.value_load(tile_e[0:1, bass.ds(t, 1)], min_val=0, max_val=E - 1)

            def up(w, p, t=None):
                e = E + p if t is None else expert(t)
                if not (isinstance(w, int) and w < 2):
                    pe.wait_ge(hid_ready, w - 1)
                pe.wait_ge(xtr_ready, w + 1)
                for blk in range(LB):
                    last = nc.tensor.matmul(up_ps[p], x_tr[p][:, blk, :],
                                            w13[:, bass.ds(e, 1), blk, :].rearrange("p a n -> p (a n)"),
                                            start=blk == 0, stop=blk == LB - 1)
                last.then_inc(up_done, 1)

            def turn_h(w, p):
                pe.wait_ge(hid_ready, w + 1)
                if not (isinstance(w, int) and w < 2):
                    pe.wait_ge(htr_ready, w - 1)
                for c in range(2):
                    last = nc.tensor.transpose(ht_ps[p][:, c, :], hid[p][:, c * HI:(c + 1) * HI], ident[:])
                last.then_inc(ht_done, 1)

            def turn_x(t, p, b, before):
                pe.wait_ge(rows_in[b], before * 16 + 16)
                if not (isinstance(t, int) and t < 2):
                    pe.wait_ge(xtr_ready, t + (SHARED - 1))
                for blk in range(LB):
                    last = nc.tensor.transpose(xt_ps[p][:, blk, :], xg[b][:, blk * P:(blk + 1) * P], ident[:])
                last.then_inc(xtr_ps, 1)

            def down_shared(w, p, tile):
                pe.wait_ge(htr_ready, w + 1)
                if p == 0:
                    at_least(pe, z_added, tile)
                for c in range(2):
                    last = nc.tensor.matmul(dn_ps[0], hid_tr[p][:, c, :], w2[:, E + p, c, :],
                                            start=p == 0 and c == 0, stop=p == 1 and c == 1)
                last.then_inc(dn_done, 1)

            def down(w, p, t):
                e = expert(t)
                if isinstance(t, int) and t < 2:
                    pe.wait_ge(z_added, UNITS)
                else:
                    pe.wait_ge(y_ready, t - 1)
                pe.wait_ge(htr_ready, w + 1)
                for c in range(2):
                    last = nc.tensor.matmul(dn_ps[p], hid_tr[p][:, c, :],
                                            w2[:, bass.ds(e, 1), c, :].rearrange("p a n -> p (a n)"),
                                            start=c == 0, stop=c == 1)
                last.then_inc(dn_done, 1)

            pe.wait_ge(wsh_in, 32 * NSH)
            up(0, 0)
            up(1, 1)
            turn_h(0, 0)
            with pe.Fori(1, UNITS - 1) as it:
                up(it * 2, 0)
                turn_h(it * 2 - 1, 1)
                down_shared(it * 2 - 2, 0, it - 1)
                up(it * 2 + 1, 1)
                turn_h(it * 2, 0)
                down_shared(it * 2 - 1, 1, it - 1)
            up(SHARED - 2, 0)
            turn_h(SHARED - 3, 1)
            down_shared(SHARED - 4, 0, UNITS - 2)
            up(SHARED - 1, 1)
            turn_h(SHARED - 2, 0)
            turn_x(0, 0, 0, 0)
            down_shared(SHARED - 3, 1, UNITS - 2)
            pe.wait_ge(w_in, 32 * E)
            pe.wait_ge(map_ready, 1)

            def routed_step(t, b, before):
                p = b % 2
                up(t + SHARED, p, t)
                turn_h(t + (SHARED - 1), 1 - p)
                if not (isinstance(t, int) and t == TILES - 1):
                    turn_x(t + 1, 1 - p, (b + 1) % DEPTH, before + 1 if b == DEPTH - 1 else before)
                if isinstance(t, int) and t < 2:
                    down_shared(t + SHARED - 2, p, UNITS - 1)
                else:
                    down(t + (SHARED - 2), p, t - 2)

            routed(pe, routed_step)
            turn_h(STEPS - 1, 1)
            down(STEPS - 2, 0, TILES - 2)
            down(STEPS - 1, 1, TILES - 1)


def kernel(x, fside_S2_0, ctx_2048, L0_xattn_k, L0_ffn_Wg, L0_ffn_W1, L0_ffn_W3, L0_ffn_W2, L0_ffn_Ws1, L0_ffn_Ws3,
           L0_ffn_Ws2):
    import concourse.bacc as bacc
    from concourse.bass_utils import run_bass_kernel_spmd

    def tiles(a):
        a = np.asarray(a).reshape(B // 2, 2, 2, HH, C, L).transpose(0, 2, 3, 1, 4, 5)
        return a.reshape(UNITS, P, L)

    ctx_u = tiles(ctx_2048)
    ctx_g = np.asarray(ctx_2048).reshape(B // 2, 2, 2, HH, C, L).transpose(0, 2, 1, 4, 3, 5)
    up_w = np.concatenate([
        np.concatenate([np.asarray(L0_ffn_W1), np.asarray(L0_ffn_Ws1).reshape(NSH, INTER, L)]),
        np.concatenate([np.asarray(L0_ffn_W3), np.asarray(L0_ffn_Ws3).reshape(NSH, INTER, L)]),
    ], axis=1)
    down_w = np.concatenate([np.asarray(L0_ffn_W2),
                             np.asarray(L0_ffn_Ws2).reshape(L, NSH, INTER).transpose(1, 0, 2)])
    arrays = {
        "x_in": tiles(x),
        "ctx_in": ctx_u,
        "ctxt_in": ctx_u.reshape(UNITS, P, LB, P)[:, :, :, ::-1].transpose(0, 3, 2, 1).reshape(UNITS, P, L),
        "ctxr_in": ctx_g.reshape(UNITS, 2 * C, HH * L),
        "k_in": L0_xattn_k,
        "bias_in": fside_S2_0,
        "wg_in": np.asarray(L0_ffn_Wg).T.reshape(LB, P, E).transpose(1, 0, 2),
        "w13_in": up_w.reshape(E + NSH, 2 * INTER, LB, P).transpose(3, 0, 2, 1),
        "w2_in": down_w.reshape(E + NSH, L, 2, HI).transpose(3, 0, 2, 1),
    }
    arrays = {n: np.ascontiguousarray(a) for n, a in arrays.items()}
    nc = bacc.Bacc("TRN2", target_bir_lowering=False, num_devices=1, dynamic_dma_scratch_size=8192)
    ins = [nc.dram_tensor(n, a.shape, mybir.dt.from_np(a.dtype), kind="ExternalInput").ap() for n, a in arrays.items()]
    out = nc.dram_tensor("out", (UNITS, P, L), F32, kind="ExternalOutput").ap()
    build(nc, *ins, out)
    got = run_bass_kernel_spmd(nc, [arrays], core_ids=[0]).results[0]["out"]
    got = np.asarray(got).reshape(B // 2, 2, HH, 2, C, L).transpose(0, 3, 1, 2, 4, 5)
    return np.ascontiguousarray(got.reshape(B, D, L))
```

```python
from contextlib import ExitStack

import numpy as np

import concourse.bass as bass
from concourse import mybir

ALU = mybir.AluOpType
ACT = mybir.ActivationFunctionType
AX_X = mybir.AxisListType.X
F32 = mybir.dt.float32
BF16 = mybir.dt.bfloat16
I32 = mybir.dt.int32
U32 = mybir.dt.uint32

P = 128
B, D, L = 16, 128, 256
H, C = 16, 8
HH = H // 2
UNITS = B * D // P
LB = L // P
KV = HH * P
EPS = 1e-5

E, TOPK, G = 16, 4, 4
GE = E // G
TOP_G = 2
INTER = 176
HI = INTER // 2
NSH = 2
TOK = B * D
REGION = TOK + P
TILES = TOK * TOPK // P + E
ROW = L + 2 * E
SW = NSH * INTER
CHUNKS = tuple((c, min(P, SW - c)) for c in range(0, SW, P))
GT = 4
GROUPS = UNITS // GT
BATCHES = 2
TB = UNITS // BATCHES
ROUTE0 = TB + 2
KEEP_WARM = 16
SCATTER0 = ROUTE0 + 5
LATE = 4
FIN = 8
DEPTH = 4

HEADS = (0, 4, 1, 5)


def build(nc, x_d, ctx_d, ctxt_d, ctxr_d, k_d, bias_d, wg_d, w13_d, w2_d, ws13_d, ws2_d, out_d):
    kpad_d = nc.dram_tensor("kpad_scratch", (H, 3 * P), F32, kind="Internal").ap()
    rows_d = nc.dram_tensor("rows_scratch", ((E + 1) * REGION, ROW), F32, kind="Internal").ap()
    y_d = nc.dram_tensor("y_scratch", (TOPK * TOK + 2 * E * P, L), F32, kind="Internal").ap()

    with ExitStack() as ctx:
        def sb(name, shape, dt=F32):
            return ctx.enter_context(nc.sbuf_tensor(name, shape, dt))

        def sem(name):
            return ctx.enter_context(nc.semaphore(name))

        bank = [ctx.enter_context(nc.psum_tensor(f"bank{i}", [P, 512], F32)) for i in range(8)]

        w13 = sb("w13", [P, E, LB, 2 * INTER])
        ws13 = sb("ws13", [P, LB, 2, SW])
        ws2 = sb("ws2", [P, len(CHUNKS), L])
        w2 = sb("w2", [HI, E, 2, L])
        wg = sb("wg", [P, LB, E])
        toep = sb("toep", [P, H, L])
        ctx_rep = sb("ctx_rep", [P, 2, HH, L])
        kv = sb("kv", [P, 2, LB, KV])
        prod = sb("prod", [P, 4, 2, L])
        ctx_n = sb("ctx_n", [P, 2, L])
        ctx_tr = sb("ctx_tr", [P, 2, LB, P])
        v = sb("v", [P, 2, L])
        vc = sb("vc", [P, 2, L])
        v_tr = sb("v_tr", [P, 2, LB, P])
        xn = sb("xn", [P, 2, L])
        xn_tr = sb("xn_tr", [P, 2, LB, P])
        resid = sb("resid", [P, UNITS, L])
        rows = sb("rows", [P, UNITS, ROW])
        xn_tr_all = sb("xn_tr_all", [P, UNITS, LB, P])
        logits = sb("logits", [P, UNITS, E])
        st1 = sb("st1", [P, 2, 16])
        st2 = sb("st2", [P, 2, 16])
        ident = sb("ident", [P, P])
        sum_i = sb("sum_i", [P, 2, 32])
        blocks = sb("blocks", [P, P])
        skip_w = sb("skip_w", [P, 2, P])
        bias_c = sb("bias_c", [P, 2])
        neg_half = sb("neg_half", [P, 1])
        before = sb("before", [P, P], BF16)
        ones = sb("ones", [P, P], BF16)
        low = sb("low", [P, G, G])
        io_e = sb("io_e", [P, E])
        io_tok = sb("io_tok", [P, UNITS])
        io_reg = sb("io_reg", [P, E])
        io_j = sb("io_j", [1, E])
        io_t = sb("io_t", [1, TILES])
        pad_row = sb("pad_row", [P, 2, ROW])
        top8 = sb("top8", [P, UNITS, 8])
        top_i = sb("top_i", [P, UNITS, 8], U32)
        sel_bf = sb("sel_bf", [P, UNITS, E], BF16)
        slot_i = sb("slot_i", [P, UNITS, TOPK], I32)
        tile_e = sb("tile_e", [1, TILES], I32)
        tile_row = sb("tile_row", [1, TILES + DEPTH], I32)
        pad_at = sb("pad_at", [1, E], I32)

        skip = vc
        zeros = prod[0:H, :, :, :].rearrange("p g h l -> p (g h l)")[:, 0:P - 1]
        kv_flat = kv[:].rearrange("p q b n -> p (q b n)")
        late = w13[:, E - LATE:E, :, :].rearrange("p e b n -> p (e b n)")
        tmp = [late, ctx_rep[:].rearrange("p q h l -> p (q h l)")]
        wide_m = kv_flat[0:1, 2048:2048 + TILES * E].rearrange("p (t e) -> p t e", e=E)
        meta = kv_flat[0:1, 2048 + TILES * E:2048 + TILES * (E + 6)].rearrange("p (i t) -> p i t", i=6)
        tf = toep[:].rearrange("p h l -> p (h l)")
        cut = [0]

        def carve(n):
            cut[0] += n
            return tf[:, cut[0] - n:cut[0]]

        xg = [carve(ROW) for _ in range(DEPTH)]
        x_tr = [carve(L).rearrange("p (b n) -> p b n", b=LB) for _ in range(2)]
        act1 = [carve(INTER) for _ in range(2)]
        hid = [carve(INTER) for _ in range(2)]
        hid_tr = [carve(2 * P)[0:HI, :].rearrange("p (b n) -> p b n", b=2) for _ in range(2)]
        y_sb = [carve(L) for _ in range(DEPTH)]
        gate_c = [carve(2) for _ in range(DEPTH)]
        act_s = [kv_flat[:, 3 * GT * P:4 * GT * P], prod[:, 0, :, :].rearrange("p h l -> p (h l)")]
        hid_s = [mem.rearrange("p (c n) -> p c n", c=len(CHUNKS))
                 for mem in (tmp[1][:, 2560:2560 + 3 * GT * P], kv_flat[:, 0:3 * GT * P])]
        dest_i = [sb(f"dest_i{i}", [P, 1], I32) for i in range(DEPTH)]
        fin = [mem[:, TOPK * L * i:TOPK * L * (i + 1)].rearrange("p (k l) -> p k l", k=TOPK)
               for mem in (ctx_rep[:].rearrange("p q h l -> p (q h l)"),
                           xn_tr_all[:].rearrange("p u b n -> p (u b n)")) for i in range(FIN // 2)]
        fin_a, fin_b, fin_o = ([kv_flat[:, (3 * i + n) * L:(3 * i + n + 1) * L] for i in range(DEPTH)]
                               for n in range(3))

        y_ps = [bank[i][:, :].rearrange("p (h l) -> p h l", h=2) for i in range(4)]
        o_ps = bank[4][:, 0:L]
        g_ps = bank[5][:, 0:L]
        tr_ps = bank[6][:, 0:L].rearrange("p (b n) -> p b n", b=LB)
        xn_ps = bank[7][:, 0:L].rearrange("p (b n) -> p b n", b=LB)
        logit_ps = bank[7][:, 0:E]
        rank_ps = [bank[i][:, at:at + TB * E].rearrange("p (t e) -> p t e", e=E) for i, at in ((5, 256), (6, 0))]
        count_ps = bank[6][:, 256:256 + UNITS * E].rearrange("p (t e) -> p t e", e=E)
        up_ps = [bank[i][:, 0:2 * INTER] for i in (0, 1)]
        ht_ps = [bank[i][0:HI, 0:2 * P].rearrange("p (b n) -> p b n", b=2) for i in (2, 3)]
        dn_ps = [bank[i][:, 0:L] for i in (4, 5)]
        xt_ps = [bank[i][:, 0:L].rearrange("p (b n) -> p b n", b=LB) for i in (6, 7)]

        wait_taken = sem("wait_taken")
        k_in, k_zero, toep_in = sem("k_in"), sem("k_zero"), [sem(f"toep_in{n}") for n in range(4)]
        bias_in, wg_in, wsh_in, w_in = sem("bias_in"), sem("wg_in"), sem("wsh_in"), sem("w_in")
        x0_in, x_in = sem("x0_in"), [sem("x_in0"), sem("x_in1")]
        ctr_in, cn_in, cr_in = ([sem(f"{n}{q}") for q in range(2)] for n in ("ctx_tr_in", "ctx_n_in", "ctx_rep_in"))
        const = sem("const")
        skipw_ready, sums_ready = sem("skipw_ready"), sem("sums_ready")
        s1a, s1b, s1c, s1d = sem("bn1"), sem("mean1"), sem("vareps1"), sem("rstd1")
        v_ready, vc_ready, vt_ps, vt_ready = sem("v_ready"), sem("vc_ready"), sem("vt_ps"), sem("vt_ready")
        kv0_ready, kv1_ready = sem("kv0_ready"), sem("kv1_ready")
        conv_done, prod_ready, even_done, sum_done = sem("conv_done"), sem("prod_ready"), sem("even_done"), sem("sum_done")
        g_done, skip_ready, xa_ready, resid_ready = sem("g_done"), sem("skip_ready"), sem("xa_ready"), sem("resid_ready")
        s2a, s2b, s2c, s2d, s2e = sem("bn2"), sem("mean2"), sem("vareps2"), sem("rstd2"), sem("shift2")
        xn_ready, row_ready, xt_done, xnt_ready, xnt_all = (
            sem("xn_ready"), sem("row_ready"), sem("xt_done"), sem("xnt_ready"), sem("xnt_all"))
        logits_done, logits_ready = sem("logits_done"), sem("logits_ready")
        r = sem("route_step")
        counted, pad_ready = sem("counted"), sem("pad_ready")
        mx_sub, exp_done, sel_ready, rank_done, slots_ready, map_ready = (
            sem("mx_sub"), sem("exp_done"), sem("sel_ready"), sem("rank_done"), sem("slots_ready"), sem("map_ready"))
        scattered, padded = sem("scattered"), sem("padded")
        s_up, s_silu, s_hid, s_down = sem("shared_up"), sem("shared_silu"), sem("shared_hid"), sem("shared_down")
        rows_in = [sem(f"rows_in{b}") for b in range(DEPTH)]
        xtr_ps, xtr_ready, up_done, silu_done, hid_ready, ht_done, htr_ready, dn_done = (
            sem("xtr_ps"), sem("xtr_ready"), sem("up_done"), sem("silu_done"), sem("hid_ready"), sem("ht_done"),
            sem("htr_ready"), sem("dn_done"))
        gate_ready, dest_ready, z_added, y_ready = sem("gate_ready"), sem("dest_ready"), sem("z_added"), sem("y_ready")
        tail_in = [sem(f"tail_in{b}") for b in range(DEPTH)]
        y_sent = [sem(f"y_sent{b}") for b in range(DEPTH)]
        fin_in = [sem(f"fin_in{b}") for b in range(FIN)]
        fa, fb, fc, fo = sem("fin_a"), sem("fin_b"), sem("fin_c"), sem("fin_o")
        out_sent = [sem(f"out_sent{b}") for b in range(DEPTH)]

        block = ctx.enter_context(nc.Block())

        def v_forward(q):
            part = v[:, q, :]
            return bass.AP(part.tensor, part.offset + P - 1, [list(part.ap[0]), [P, LB], [-1, P]])

        def at_least(eng, s, n):
            if isinstance(n, int) and n <= 0:
                return
            eng.wait_ge(s, n)

        def part(eng):
            eng.sem_inc(wait_taken, 1)

        def units(eng, step, between):
            for u in range(4):
                step(u, u % 2, u // 2 + 1 + u % 2, u == 0, False)
            with eng.Fori(2, ROUTE0 // 2) as it:
                step(it * 2, 0, it + 1, False, False)
                step(it * 2 + 1, 1, it + 2, False, False)
            for u in range(ROUTE0, UNITS):
                between(u)
                step(u, u % 2, u // 2 + 1 + u % 2, False, u == UNITS - 1)
            between(UNITS)

        def routed(eng, step):
            for t in range(2 * DEPTH):
                step(t, t % DEPTH, t // DEPTH)
            with eng.Fori(2, TILES // DEPTH - 1) as it:
                for b in range(DEPTH):
                    step(it * DEPTH + b, b, it)
            for b in range(DEPTH):
                step(TILES - DEPTH + b, b, TILES // DEPTH - 1)

        def tail_tile(t):
            return isinstance(t, int) and t > TILES - DEPTH

        C_IDENT, C_SUM, C_BLOCKS, C_ALL = 3, 4, 7, 18

        @block.sync
        def _(sp):
            def load(u, q, what=None):
                late = not (isinstance(u, int) and u < 2)
                if late:
                    sp.dma_start(resid[:, bass.ds(u, 1), :].rearrange("p a l -> p (a l)"),
                                 x_d[bass.ds(u, 1)].rearrange("a p l -> (a p) l")).then_inc(x_in[q], 16)
                    sp.wait_ge(kv0_ready, u - 1)
                    sp.wait_ge(kv1_ready, u - 1)
                if what in ("tr", None):
                    sp.dma_start(ctx_tr[:, q, :, :].rearrange("p b n -> p (b n)"),
                                 ctxt_d[bass.ds(u, 1)].rearrange("a p n -> (a p) n")).then_inc(ctr_in[q], 16)
                if late:
                    sp.wait_ge(skip_ready, u - 1)
                    sp.wait_ge(vc_ready, u - 1)
                if what in ("n", None):
                    sp.dma_start(ctx_n[:, q, :],
                                 ctx_d[bass.ds(u, 1)].rearrange("a p l -> (a p) l")).then_inc(cn_in[q], 16)
                if late:
                    sp.wait_ge(prod_ready, (u - 1) * 4)
                src = ctxr_d[bass.ds(u, 1)].rearrange("a g n -> (a g) n")
                src = src.unsqueeze(1).to_broadcast([2 * C, C, HH * L])
                if what in ("rep", None):
                    sp.dma_start(ctx_rep[:, q, :, :].rearrange("p h l -> p (h l)"), src).then_inc(cr_in[q], 16)

            def load_expert(e, landed):
                sp.dma_start(w13[:, bass.ds(e, 1), :, :].rearrange("p a b n -> p (a b n)"),
                             w13_d[:, bass.ds(e, 1), :, :].rearrange("p a b n -> p (a b n)")).then_inc(landed, 16)
                sp.dma_start(w2[:, bass.ds(e, 1), :, :].rearrange("p a b n -> p (a b n)"),
                             w2_d[:, bass.ds(e, 1), :, :].rearrange("p a b n -> p (a b n)")).then_inc(landed, 16)

            sp.dma_start(resid[:, 0:2, :], x_d[0:2].rearrange("u p l -> p u l")).then_inc(x0_in, 16)
            sp.dma_start(kpad_d[:, P - 1:P - 1 + L], k_d).then_inc(k_in, 16)
            sp.wait_ge(k_zero, 1)
            sp.dma_start(kpad_d[:, 0:P - 1], zeros).then_inc(k_in, 16)
            load(0, 0, "tr")
            load(0, 0, "n")
            sp.wait_ge(k_in, 32)

            def load_toep(q):
                for part in range(2):
                    h = q * HH + part * HH // 2
                    first = kpad_d[h:h + HH // 2, 0:L]
                    window = bass.AP(first.tensor, first.offset, [[1, P], [3 * P, HH // 2], [1, L]])
                    sp.dma_start(toep[:, h:h + HH // 2, :], window).then_inc(toep_in[2 * q + part], 16)

            load_toep(0)
            load(0, 0, "rep")
            sp.dma_start(bias_c[:], bias_d).then_inc(bias_in, 16)
            load(1, 1, "tr")
            load(1, 1, "n")
            load_toep(1)
            load(1, 1, "rep")
            sp.dma_start(wg[:], wg_d).then_inc(wg_in, 16)
            with sp.Fori(1, (E - LATE) // 2) as it:
                load(it * 2, 0)
                load_expert(it * 2, w_in)
                load(it * 2 + 1, 1)
                load_expert(it * 2 + 1, w_in)
            for u in range(E - LATE, UNITS):
                load(u, u % 2)
                if u == E - LATE:
                    sp.dma_start(ws13[:], ws13_d).then_inc(wsh_in, 16)
                elif u == E - LATE + 1:
                    sp.dma_start(ws2[:, 0:2, :], ws2_d[0:2 * P].rearrange("(c p) l -> p c l", p=P)).then_inc(wsh_in, 16)
                    sp.dma_start(ws2[0:SW - 2 * P, 2, :], ws2_d[2 * P:]).then_inc(wsh_in, 16)
                else:
                    load_expert(u - (E - LATE + 2), w_in)
            sp.wait_ge(slots_ready, 1)
            with sp.Fori(E - LATE, E) as e:
                load_expert(e, w_in)
            sp.wait_ge(pad_ready, 1)
            with sp.Fori(0, E) as e:
                at = sp.value_load(pad_at[0:1, bass.ds(e, 1)], min_val=0, max_val=E * REGION)
                sp.dma_start(rows_d[bass.ds(at, P)], pad_row[:, 0, :]).then_inc(padded, 16)
            sp.dma_start(rows_d[E * REGION:E * REGION + P], pad_row[:, 1, :]).then_inc(padded, 16)
            sp.wait_ge(map_ready, 1)
            sp.wait_ge(padded, 16 * (E + 1))
            sp.wait_ge(scattered, 16 * UNITS * TOPK)

            def gather(t, b, before):
                if tail_tile(t):
                    at = sp.value_load(tile_row[0:1, t:t + 1], min_val=0, max_val=E * REGION)
                    sp.dma_start(rows[:, b, :], rows_d[bass.ds(at, P)]).then_inc(tail_in[b], 16)
                    return
                if not (isinstance(t, int) and t < DEPTH):
                    sp.wait_ge(xtr_ps, t - (DEPTH - 1))
                    sp.wait_ge(dest_ready, t - (DEPTH - 1))
                at = sp.value_load(tile_row[0:1, bass.ds(t, 1)], min_val=0, max_val=E * REGION)
                sp.dma_start(xg[b], rows_d[bass.ds(at, P)]).then_inc(rows_in[b], 16)

            routed(sp, gather)
            sends = [sp.value_load(tile_row[0:1, TILES + b:TILES + b + 1], min_val=16 * (TOPK * UNITS // DEPTH),
                                   max_val=16 * (TILES // DEPTH)) for b in range(DEPTH)]
            for b in range(DEPTH):
                sp.wait_ge(y_sent[b], sends[b])
            y_v = y_d[0:TOPK * TOK].rearrange("(k n) l -> n k l", k=TOPK)

            def final(u):
                if u >= FIN:
                    sp.wait_ge(fa, u - FIN + 1)
                    sp.wait_ge(fb, u - FIN + 1)
                sp.dma_start(fin[u % FIN], y_v[u * P:(u + 1) * P]).then_inc(fin_in[u % FIN], 16)

            def store(u):
                sp.wait_ge(fo, u + 1)
                sp.dma_start(out_d[u], fin_o[u % DEPTH]).then_inc(out_sent[u % DEPTH], 16)

            for u in range(FIN):
                sp.wait_ge(y_ready, TILES - 8 + u)
                final(u)
            for u in range(FIN, UNITS):
                final(u)
                store(u - FIN)
            for u in range(UNITS - FIN, UNITS):
                store(u)
            for b in range(DEPTH):
                sp.wait_ge(out_sent[b], 16 * (UNITS // DEPTH))
                sp.wait_ge(y_sent[b], 16 * (TILES // DEPTH))

        @block.scalar
        def _(act):
            def copy_v(u, q):
                act.wait_ge(vt_ps, u + 1)
                if not (isinstance(u, int) and u < 2):
                    act.wait_ge(kv0_ready, u - 1)
                    act.wait_ge(kv1_ready, u - 1)
                nc.scalar.activation(v_tr[:, q, :, :], tr_ps, ACT.Copy).then_inc(vt_ready, 1)

            def normal(u, q):
                act.wait_ge(s2e, u + 1)
                if not (isinstance(u, int) and u < 2):
                    act.wait_ge(xt_done, u - 1)
                part(act)
                nc.scalar.activation(xn[:, q, :], resid[:, bass.ds(u, 1), :].rearrange("p a l -> p (a l)"),
                                     ACT.Identity, bias=st2[:, q, 10:11], scale=st2[:, q, 9:10]).then_inc(xn_ready, 1)
                nc.scalar.activation(rows[:, bass.ds(u, 1), 0:L].rearrange("p a l -> p (a l)"),
                                     resid[:, bass.ds(u, 1), :].rearrange("p a l -> p (a l)"),
                                     ACT.Identity, bias=st2[:, q, 10:11], scale=st2[:, q, 9:10]).then_inc(row_ready, 1)

            def copy_xn(u, q):
                act.wait_ge(xt_done, u + 1)
                if not (isinstance(u, int) and u < 2):
                    act.wait_ge(logits_done, u - 1)
                nc.scalar.activation(xn_tr[:, q, :, :], xn_ps, ACT.Copy).then_inc(xnt_ready, 1)
                nc.scalar.activation(xn_tr_all[:, bass.ds(u, 1), :, :].rearrange("p a b n -> p (a b) n"), xn_ps,
                                     ACT.Copy).then_inc(xnt_all, 1)

            def copy_logits(u):
                act.wait_ge(logits_done, u + 1)
                part(act)
                nc.scalar.activation(logits[:, bass.ds(u, 1), :].rearrange("p a e -> p (a e)"), logit_ps,
                                     ACT.Copy).then_inc(logits_ready, 1)

            def step(u, q, landed, first, last):
                second = not (isinstance(u, int) and u < 2)
                if not last:
                    copy_v(u + 1, 1 - q)
                if second:
                    copy_xn(u - 2, q)
                if second:
                    copy_logits(u - 2)
                if not first:
                    normal(u - 1, 1 - q)

            copy_v(0, 0)

            def exponentials(b):
                act.wait_ge(mx_sub, b + 1)
                nc.scalar.activation(tmp[b][:, TB * E:2 * TB * E], tmp[b][:, 0:TB * E], ACT.Exp).then_inc(exp_done, 1)

            def between(u):
                if u == ROUTE0 + 1:
                    exponentials(0)

            units(act, step, between)

            def src_tr(w, p):
                if not (isinstance(w, int) and w < 2):
                    act.wait_ge(up_done, w - 1)
                act.wait_ge(xtr_ps, w + 1)
                nc.scalar.activation(x_tr[p], xt_ps[p], ACT.Copy).then_inc(xtr_ready, 1)

            def silu(w, p):
                act.wait_ge(up_done, w + 1)
                if not (isinstance(w, int) and w < 2):
                    act.wait_ge(hid_ready, w - 1)
                nc.scalar.activation(act1[p], up_ps[p][:, 0:INTER], ACT.Silu).then_inc(silu_done, 1)

            def store_y(t, p, b, before):
                act.wait_ge(dn_done, t + 1)
                at_least(act, y_sent[b], before * 16)
                nc.scalar.activation(y_sb[b], dn_ps[p], ACT.Copy).then_inc(y_ready, 1)

            def silu_shared(s):
                rows_c = CHUNKS[s % len(CHUNKS)][1]
                act.wait_ge(s_up, s + 1)
                if s >= 2:
                    act.wait_ge(s_hid, s - 1)
                nc.scalar.activation(act_s[s % 2][0:rows_c, :], bank[2 * (s % 2)][0:rows_c, :], ACT.Silu
                                     ).then_inc(s_silu, 1)

            act.wait_ge(sum_done, UNITS)
            silu_shared(0)
            copy_xn(UNITS - 2, 0)
            copy_logits(UNITS - 2)
            normal(UNITS - 1, 1)
            silu_shared(1)
            copy_xn(UNITS - 1, 1)
            silu_shared(2)
            copy_logits(UNITS - 1)
            exponentials(1)
            nc.scalar.preload_act_table(ACT.Silu)
            for s in range(3, GROUPS * len(CHUNKS)):
                silu_shared(s)
            src_tr(0, 0)

            def routed_step(t, b, before):
                p = b % 2
                silu(t, p)
                if not (isinstance(t, int) and t == TILES - 1):
                    src_tr(t + 1, 1 - p)
                if not (isinstance(t, int) and t < 2):
                    store_y(t - 2, p, (b - 2) % DEPTH, before if b >= 2 else before - 1)

            routed(act, routed_step)
            store_y(TILES - 2, 0, DEPTH - 2, TILES // DEPTH - 1)
            store_y(TILES - 1, 1, DEPTH - 1, TILES // DEPTH - 1)

        @block.gpsimd
        def _(pool):
            n = [0]

            def done(ins):
                n[0] += 1
                ins.then_inc(const, 1)
                pool.wait_ge(const, n[0])

            nc.gpsimd.memset(zeros, 0.0).then_inc(k_zero, 1)
            done(nc.gpsimd.memset(neg_half[:], -0.5))
            done(nc.gpsimd.memset(ident[:], 0.0))
            done(nc.gpsimd.affine_select(out=ident[:], in_=ident[:], compare_op=ALU.not_equal, fill=1.0, base=0,
                                         pattern=[[-1, P]], channel_multiplier=1))
            done(nc.gpsimd.memset(sum_i[:], 0.0))
            done(nc.gpsimd.memset(blocks[:], 1.0))
            bv = blocks[:].rearrange("p (n j) -> p n j", j=C)
            done(nc.gpsimd.affine_select(out=bv, in_=bv, compare_op=ALU.is_ge, fill=0.0, base=0,
                                         pattern=[[-C, P // C], [0, C]], channel_multiplier=1))
            done(nc.gpsimd.affine_select(out=bv, in_=bv, compare_op=ALU.is_ge, fill=0.0, base=C - 1,
                                         pattern=[[C, P // C], [0, C]], channel_multiplier=-1))

            def v_stats(u, q):
                pool.wait_ge(s1c, u + 1)
                nc.gpsimd.tensor_tensor(st1[:, q, 9:10], st1[:, q, 8:9], neg_half[:], ALU.pow).then_inc(s1d, 1)

            def v_ctx(u, q, landed):
                pool.wait_ge(v_ready, u + 1)
                if not (isinstance(u, int) and u < 2):
                    pool.wait_ge(resid_ready, u - 1)
                pool.wait_ge(cn_in[q], landed * 16)
                nc.gpsimd.tensor_tensor(vc[:, q, :].rearrange("p (b n) -> p b n", b=LB), v_forward(q),
                                        ctx_n[:, q, :].rearrange("p (b n) -> p b n", b=LB), ALU.mult).then_inc(vc_ready, 1)

            def kv_block1(u, q, landed):
                pool.wait_ge(vt_ready, u + 1)
                if not (isinstance(u, int) and u < 2):
                    pool.wait_ge(conv_done, 4 * (u - 1))
                pool.wait_ge(ctr_in[q], landed * 16)
                nc.gpsimd.tensor_tensor(
                    kv[:, q, 1, :].rearrange("p (g i j) -> p g i j", i=C, j=C),
                    v_tr[:, q, 1, :].rearrange("p (g i) -> p g i", i=C).unsqueeze(3).to_broadcast([P, 2 * HH, C, C]),
                    ctx_tr[:, q, 1, :].rearrange("p (g j) -> p g j", j=C).unsqueeze(2).to_broadcast([P, 2 * HH, C, C]),
                    ALU.mult).then_inc(kv1_ready, 1)

            def x_work(u, q):
                pool.wait_ge(xa_ready, u + 1)
                pool.wait_ge(skip_ready, u + 1)
                rv = resid[:, bass.ds(u, 1), :].rearrange("p a l -> p (a l)")
                nc.gpsimd.tensor_tensor(rv, rv, skip[:, q, :], ALU.add).then_inc(resid_ready, 1)

            def x_stats(u, q):
                pool.wait_ge(s2c, u + 1)
                nc.gpsimd.tensor_tensor(st2[:, q, 9:10], st2[:, q, 8:9], neg_half[:], ALU.pow).then_inc(s2d, 1)

            def step(u, q, landed, first, last):
                if not last:
                    v_stats(u + 1, 1 - q)
                if not first:
                    x_work(u - 1, 1 - q)
                if not last:
                    v_ctx(u + 1, 1 - q, landed)
                if not last:
                    kv_block1(u + 1, 1 - q, landed)
                if not first:
                    x_stats(u - 1, 1 - q)

            def scatter(u):
                pool.wait_ge(slots_ready, u // TB + 1)
                pool.wait_ge(row_ready, u + 1)
                for k in range(TOPK):
                    pool.indirect_dma_start(
                        rows_d, bass.IndirectOffsetOnAxis(ap=slot_i[:, u, k:k + 1].bitcast(U32), axis=0),
                        rows[:, u, :], None).then_inc(scattered, 16)

            def routing_constants():
                done(nc.gpsimd.memset(ones[:], 1.0))
                done(nc.gpsimd.affine_select(out=before[:], in_=ones[:], compare_op=ALU.is_gt, fill=0.0, base=0,
                                             pattern=[[1, P]], channel_multiplier=-1))
                done(nc.gpsimd.memset(low[:], 1.0))
                done(nc.gpsimd.affine_select(out=low[:], in_=low[:], compare_op=ALU.is_gt, fill=0.0, base=0,
                                             pattern=[[1, G], [-1, G]], channel_multiplier=0))
                exact = dict(allow_small_or_imprecise_dtypes=True)
                done(nc.gpsimd.iota(io_e[:], [[1, E]], base=0, channel_multiplier=0, **exact))
                done(nc.gpsimd.iota(io_tok[:], [[P, UNITS]], base=0, channel_multiplier=1, **exact))
                done(nc.gpsimd.iota(io_reg[:], [[REGION, E]], base=0, channel_multiplier=0, **exact))
                done(nc.gpsimd.iota(io_j[:], [[P, E]], base=0, channel_multiplier=0, **exact))
                done(nc.gpsimd.iota(io_t[:], [[1, TILES]], base=0, channel_multiplier=0, **exact))
                done(nc.gpsimd.memset(pad_row[:, :, 0:L + E], 0.0))
                done(nc.gpsimd.iota(pad_row[:, :, L + E:], [[E * P, 2], [P, E]], base=TOPK * TOK, channel_multiplier=1,
                                    **exact))

            def between(u):
                if u == ROUTE0:
                    routing_constants()
                if u >= SCATTER0:
                    scatter(u - SCATTER0)

            v_stats(0, 0)
            kv_block1(0, 0, 1)
            v_ctx(0, 0, 1)
            units(pool, step, between)
            x_work(UNITS - 1, 1)
            x_stats(UNITS - 1, 1)
            for u in range(UNITS + 1 - SCATTER0, UNITS):
                scatter(u)

            def send(t, b):
                pool.wait_ge(y_ready, t + 1)
                pool.wait_ge(dest_ready, t + 1)
                part(pool)
                pool.indirect_dma_start(
                    y_d, bass.IndirectOffsetOnAxis(ap=dest_i[b][:, 0:1].bitcast(U32), axis=0),
                    y_sb[b], None).then_inc(y_sent[b], 16)

            with pool.Fori(0, TILES // DEPTH) as it:
                for b in range(DEPTH):
                    send(it * DEPTH + b, b)

            pool.wait_ge(z_added, UNITS)
            for u in range(UNITS):
                pool.wait_ge(fin_in[u % FIN], 16 * (u // FIN + 1))
                if u >= DEPTH:
                    pool.wait_ge(fo, u - DEPTH + 1)
                nc.gpsimd.tensor_tensor(fin_b[u % DEPTH], fin[u % FIN][:, 3, :], resid[:, u, :],
                                        ALU.add).then_inc(fb, 1)

        @block.vector
        def _(dve):
            def tile(u):
                return resid[:, bass.ds(u, 1), :].rearrange("p a l -> p (a l)")

            def stats1(u, q, landed):
                if isinstance(u, int) and u < 2:
                    dve.wait_ge(x0_in, 16)
                else:
                    dve.wait_ge(x_in[q], (landed - 1) * 16)
                    part(dve)
                nc.vector.bn_stats(st1[:, q, 0:6], tile(u)).then_inc(s1a, 1)
                dve.wait_ge(s1a, u + 1)
                part(dve)
                nc.vector.bn_aggr(st1[:, q, 6:8], st1[:, q, 0:6]).then_inc(s1b, 1)
                dve.wait_ge(s1b, u + 1)
                nc.vector.tensor_scalar(st1[:, q, 8:9], st1[:, q, 7:8], EPS, None, ALU.add).then_inc(s1c, 1)

            def norm1(u, q):
                dve.wait_ge(s1d, u + 1)
                if not (isinstance(u, int) and u < 2):
                    dve.wait_ge(vt_ps, u - 1)
                    dve.wait_ge(vc_ready, u - 1)
                nc.vector.tensor_scalar(v_forward(q), tile(u).rearrange("p (b n) -> p b n", b=LB), st1[:, q, 6:7], st1[:, q, 9:10],
                                        ALU.subtract, ALU.mult).then_inc(v_ready, 1)

            def kv_block0(u, q, landed):
                dve.wait_ge(ctr_in[q], landed * 16)
                dve.wait_ge(vt_ready, u + 1)
                if not (isinstance(u, int) and u < 2):
                    dve.wait_ge(conv_done, 4 * (u - 1))
                nc.vector.tensor_tensor(
                    kv[:, q, 0, :].rearrange("p (g i j) -> p g i j", i=C, j=C),
                    v_tr[:, q, 0, :].rearrange("p (g i) -> p g i", i=C).unsqueeze(3).to_broadcast([P, 2 * HH, C, C]),
                    ctx_tr[:, q, 0, :].rearrange("p (g j) -> p g j", j=C).unsqueeze(2).to_broadcast([P, 2 * HH, C, C]),
                    ALU.mult).then_inc(kv0_ready, 1)

            def product(u, q, g, landed, first):
                dve.wait_ge(conv_done, 4 * u + g + 1)
                if g == 0:
                    dve.wait_ge(cr_in[q], (landed - q) * 16)
                if not first:
                    dve.wait_ge(even_done if g < 2 else sum_done, u)
                h0 = HEADS[g]
                nc.vector.tensor_tensor(prod[:, g, :, :], y_ps[g], ctx_rep[:, q, h0:h0 + 3:2, :],
                                        ALU.mult).then_inc(prod_ready, 1)

            def add_x(u, q):
                dve.wait_ge(sum_done, u + 1)
                nc.vector.tensor_tensor(tile(u), o_ps, tile(u), ALU.add).then_inc(xa_ready, 1)

            def skip_term(u, q):
                dve.wait_ge(g_done, u + 1)
                if not (isinstance(u, int) and u < 2):
                    dve.wait_ge(resid_ready, u - 1)
                nc.vector.tensor_tensor(skip[:, q, :], g_ps, ctx_n[:, q, :], ALU.mult).then_inc(skip_ready, 1)

            def stats2(u, q):
                dve.wait_ge(resid_ready, u + 1)
                part(dve)
                nc.vector.bn_stats(st2[:, q, 0:6], tile(u)).then_inc(s2a, 1)
                dve.wait_ge(s2a, u + 1)
                if not (isinstance(u, int) and u < 2):
                    dve.wait_ge(row_ready, u - 1)
                part(dve)
                nc.vector.bn_aggr(st2[:, q, 6:8], st2[:, q, 0:6]).then_inc(s2b, 1)
                dve.wait_ge(s2b, u + 1)
                nc.vector.tensor_scalar(st2[:, q, 8:9], st2[:, q, 7:8], EPS, None, ALU.add).then_inc(s2c, 1)

            def shift2(u, q):
                dve.wait_ge(s2d, u + 1)
                nc.vector.scalar_tensor_tensor(st2[:, q, 10:11], st2[:, q, 6:7], -1.0, st2[:, q, 9:10],
                                               ALU.mult, ALU.mult).then_inc(s2e, 1)

            def step(u, q, landed, first, last):
                if not last:
                    stats1(u + 1, 1 - q, landed)
                    norm1(u + 1, 1 - q)
                product(u, q, 0, landed, first)
                if isinstance(u, int) and u >= ROUTE0:
                    beside_early(u)
                if not first:
                    add_x(u - 1, 1 - q)
                product(u, q, 1, landed, first)
                if first:
                    dve.wait_ge(bias_in, 16)
                    dve.wait_ge(const, C_BLOCKS)
                    for i in range(2):
                        nc.vector.tensor_scalar(skip_w[:, i, :], blocks[:], bias_c[:, i:i + 1], None, ALU.mult
                                                ).then_inc(skipw_ready, 1)
                if isinstance(u, int) and u == ROUTE0 + 3:
                    dve.wait_ge(g_done, u + 1)
                    slot_of_expert(0)
                skip_term(u, q)
                if not first:
                    stats2(u - 1, 1 - q)
                if not last:
                    kv_block0(u + 1, 1 - q, landed)
                product(u, q, 2, landed, first)
                if isinstance(u, int) and u >= ROUTE0:
                    beside_late(u)
                product(u, q, 3, landed, first)
                if not first:
                    shift2(u - 1, 1 - q)

            stats1(0, 0, 1)
            norm1(0, 0)
            dve.wait_ge(const, C_SUM)
            for par in range(2):
                nc.vector.tensor_reduce(sum_i[:, par, 16 * par:16 * par + 16].rearrange("p (b j) -> p b j", j=C),
                                        ident[:].rearrange("p (b i j) -> p b j i", b=2, i=C), AX_X, ALU.add
                                        ).then_inc(sums_ready, 1)
            kv_block0(0, 0, 1)

            n = [0]

            def then(ins):
                n[0] += 1
                ins.then_inc(r, 1)
                dve.wait_ge(r, n[0])

            NE = TB * E

            def flat(b, i):
                return tmp[b][:, i * NE:(i + 1) * NE]

            def te(b, i):
                return flat(b, i).rearrange("p (t e) -> p t e", e=E)

            def tgg(b, i):
                return flat(b, i).rearrange("p (t g o) -> p t g o", g=G, o=G)

            def small(b, at, width):
                return tmp[b][:, 10 * NE + at:10 * NE + at + width]

            def onehot(b):
                return tmp[b][:, 12 * NE:16 * NE].rearrange("p (t k e) -> p t k e", t=TB, k=TOPK)

            def wide(b):
                return tmp[b][:, 16 * NE:20 * NE]

            def tiles_of(b):
                return slice(b * TB, (b + 1) * TB)

            def less_max(b):
                lg = logits[:, tiles_of(b), :]
                mx = small(b, 0, TB)
                dve.wait_ge(logits_ready, (b + 1) * TB)
                then(nc.vector.tensor_reduce(mx, lg, AX_X, ALU.max))
                nc.vector.tensor_tensor(te(b, 0), lg, mx.unsqueeze(2).to_broadcast([P, TB, E]),
                                        ALU.subtract).then_inc(mx_sub, 1)

            def scores(b):
                total, part_of = small(b, TB, TB), small(b, 2 * TB, TB)
                dve.wait_ge(exp_done, b + 1)
                then(nc.vector.tensor_reduce(total, te(b, 1), AX_X, ALU.add))
                then(nc.vector.reciprocal(part_of, total))
                then(nc.vector.tensor_tensor(te(b, 3), te(b, 1), part_of.unsqueeze(2).to_broadcast([P, TB, E]),
                                             ALU.mult))

            def groups(b):
                best = small(b, 32, TB * G)
                then(nc.vector.tensor_reduce(best, flat(b, 3).rearrange("p (n i) -> p n i", i=GE), AX_X, ALU.max))
                gm = best.rearrange("p (t g) -> p t g", g=G)
                other = gm.unsqueeze(2).to_broadcast([P, TB, G, G])
                own = gm.unsqueeze(3).to_broadcast([P, TB, G, G])
                then(nc.vector.tensor_tensor(tgg(b, 4), other, own, ALU.is_equal))
                then(nc.vector.tensor_tensor(tgg(b, 5), other, own, ALU.is_gt))
                dve.wait_ge(const, C_ALL)
                then(nc.vector.tensor_tensor(tgg(b, 4), tgg(b, 4), low[:].unsqueeze(1).to_broadcast([P, TB, G, G]),
                                             ALU.mult))
                then(nc.vector.tensor_tensor(tgg(b, 5), tgg(b, 4), tgg(b, 5), ALU.add))

            def keep_groups(b):
                rank, top = small(b, 64, TB * G), small(b, 96, TB * G)
                then(nc.vector.tensor_reduce(rank, flat(b, 5).rearrange("p (n o) -> p n o", o=G), AX_X, ALU.add))
                then(nc.vector.tensor_scalar(top, rank, TOP_G - 0.5, None, ALU.is_lt))
                kept = top.unsqueeze(2).to_broadcast([P, TB * G, GE])
                ng = lambda i: flat(b, i).rearrange("p (n i) -> p n i", i=GE)
                then(nc.vector.tensor_tensor(ng(4), ng(3), kept, ALU.mult))
                then(nc.vector.scalar_tensor_tensor(ng(5), kept, -1.0, ng(4), ALU.add, ALU.add))

            def choose(b):
                for t in range(TB):
                    last = nc.vector.max(top8[:, b * TB + t, :], te(b, 5)[:, t, :])
                then(last)
                for t in range(TB):
                    last = nc.vector.max_index(top_i[:, b * TB + t, :], top8[:, b * TB + t, :], te(b, 5)[:, t, :])
                then(last)

            def choices(b):
                idx_f = small(b, 128, TB * TOPK).rearrange("p (t k) -> p t k", k=TOPK)
                then(nc.vector.tensor_copy(idx_f, top_i[:, tiles_of(b), 0:TOPK]))
                then(nc.vector.tensor_tensor(onehot(b), idx_f.unsqueeze(3).to_broadcast([P, TB, TOPK, E]),
                                             io_e[:].unsqueeze(1).unsqueeze(1).to_broadcast([P, TB, TOPK, E]),
                                             ALU.is_equal))

            def marks(b):
                then(nc.vector.tensor_tensor(te(b, 4), onehot(b)[:, :, 0, :], onehot(b)[:, :, 1, :], ALU.add))
                then(nc.vector.tensor_tensor(te(b, 6), onehot(b)[:, :, 2, :], onehot(b)[:, :, 3, :], ALU.add))
                then(nc.vector.tensor_tensor(te(b, 7), te(b, 4), te(b, 6), ALU.add))
                nc.vector.tensor_copy(sel_bf[:, tiles_of(b), :], te(b, 7)).then_inc(sel_ready, 1)

            def places(b):
                out = rows[:, tiles_of(b), :]
                then(nc.vector.tensor_tensor(out[:, :, L:L + E], te(b, 7), te(b, 3), ALU.mult))
                then(nc.vector.scalar_tensor_tensor(te(b, 8), onehot(b)[:, :, 2, :], 2.0, onehot(b)[:, :, 1, :],
                                                    ALU.mult, ALU.add))
                then(nc.vector.scalar_tensor_tensor(te(b, 9), onehot(b)[:, :, 3, :], 3.0, te(b, 8), ALU.mult, ALU.add))
                then(nc.vector.scalar_tensor_tensor(out[:, :, L + E:], te(b, 9), float(TOK),
                                                    io_tok[:, tiles_of(b)].unsqueeze(2).to_broadcast([P, TB, E]),
                                                    ALU.mult, ALU.add))

            def slot_of_expert(b):
                dve.wait_ge(rank_done, b + 1)
                then(nc.vector.tensor_tensor(te(b, 2), rank_ps[b],
                                             io_reg[:].unsqueeze(1).to_broadcast([P, TB, E]), ALU.add))

            def slots(b):
                wv = wide(b).rearrange("p (t k e) -> p t k e", k=TOPK, e=E)
                then(nc.vector.tensor_tensor(wv, onehot(b), te(b, 2).unsqueeze(2).to_broadcast([P, TB, TOPK, E]),
                                             ALU.mult))
                slot_f = small(b, 160, TB * TOPK)
                then(nc.vector.tensor_reduce(slot_f, wide(b).rearrange("p (n e) -> p n e", e=E), AX_X, ALU.add))
                nc.vector.tensor_copy(slot_i[:, tiles_of(b), :].rearrange("p t k -> p (t k)"), slot_f
                                      ).then_inc(slots_ready, 1)

            cnt, tiles_e = meta[:, 0, 0:E], meta[:, 0, E:2 * E]
            upto = [meta[:, 1, 0:E], meta[:, 1, E:2 * E]]

            def rows_per_expert():
                dve.wait_ge(counted, 1)
                then(nc.vector.tensor_reduce(cnt, count_ps[0:1].rearrange("p t e -> p e t"), AX_X, ALU.add))
                nc.vector.tensor_tensor(pad_at[:], cnt, io_reg[0:1, :], ALU.add).then_inc(pad_ready, 1)

            def tiles_per_expert():
                jj = wide_m[:, 0:E, :]
                then(nc.vector.tensor_tensor(jj, cnt.unsqueeze(2).to_broadcast([1, E, E]),
                                             io_j[:].unsqueeze(1).to_broadcast([1, E, E]), ALU.is_gt))
                then(nc.vector.tensor_reduce(tiles_e, jj, AX_X, ALU.add))
                then(nc.vector.tensor_copy(upto[0], tiles_e))

            def running_tiles():
                for i, sh in enumerate((1, 2, 4, 8)):
                    a, b = upto[i % 2], upto[1 - i % 2]
                    then(nc.vector.tensor_copy(b[:, 0:sh], a[:, 0:sh]))
                    then(nc.vector.tensor_tensor(b[:, sh:], a[:, sh:], a[:, 0:E - sh], ALU.add))

            def tile_owner():
                then(nc.vector.tensor_tensor(wide_m, io_t[:].unsqueeze(2).to_broadcast([1, TILES, E]),
                                             upto[0].unsqueeze(1).to_broadcast([1, TILES, E]), ALU.is_ge))

            def count_owner():
                then(nc.vector.tensor_reduce(meta[:, 2, :], wide_m, AX_X, ALU.add))

            def tiles_before():
                then(nc.vector.tensor_tensor(wide_m, wide_m, tiles_e.unsqueeze(1).to_broadcast([1, TILES, E]),
                                             ALU.mult))

            def count_before():
                then(nc.vector.tensor_reduce(meta[:, 3, :], wide_m, AX_X, ALU.add))

            def first_rows():
                then(nc.vector.tensor_tensor(meta[:, 4, :], io_t[:], meta[:, 3, :], ALU.subtract))
                then(nc.vector.tensor_scalar(meta[:, 5, :], meta[:, 2, :], float(REGION), None, ALU.mult))
                then(nc.vector.scalar_tensor_tensor(meta[:, 3, :], meta[:, 4, :], float(P), meta[:, 5, :],
                                                    ALU.mult, ALU.add))
                then(nc.vector.tensor_scalar(tile_row[:, 0:TILES], meta[:, 3, :], float(E * REGION), None, ALU.min))

            def last_send():
                holds = meta[:, 5, :]
                then(nc.vector.tensor_tensor(holds, io_t[:], upto[0][:, E - 1:E].to_broadcast([1, TILES]), ALU.is_lt))
                then(nc.vector.tensor_reduce(meta[:, 4, 0:DEPTH], holds.rearrange("p (j b) -> p b j", b=DEPTH),
                                             AX_X, ALU.add))
                then(nc.vector.tensor_scalar(tile_row[:, TILES:], meta[:, 4, 0:DEPTH], 16.0, None, ALU.mult))

            def tile_experts():
                then(nc.vector.tensor_scalar(meta[:, 5, :], meta[:, 2, :], E - 0.5, None, ALU.is_gt))
                then(nc.vector.scalar_tensor_tensor(meta[:, 3, :], meta[:, 4, :], float(-E), meta[:, 5, :],
                                                    ALU.add, ALU.mult))
                nc.vector.tensor_tensor(tile_e[:], meta[:, 3, :], meta[:, 2, :], ALU.add).then_inc(map_ready, 1)

            def beside_early(u):
                if u == ROUTE0 + 1:
                    scores(0)
                if u == ROUTE0 + 2:
                    choose(0)
                if u == ROUTE0 + 3:
                    places(0)

            def beside_late(u):
                if u == ROUTE0:
                    less_max(0)
                if u == ROUTE0 + 1:
                    groups(0)
                    keep_groups(0)
                if u == ROUTE0 + 2:
                    choices(0)
                    marks(0)
                if u == ROUTE0 + 3:
                    slots(0)

            units(dve, step, lambda u: None)

            def hidden(t, p, b):
                dve.wait_ge(silu_done, t + 1)
                if not (isinstance(t, int) and t < 2):
                    dve.wait_ge(ht_done, t - 1)
                dve.wait_ge(gate_ready, t + 1)
                nc.vector.scalar_tensor_tensor(hid[p], act1[p], gate_c[b][:, 0:1], up_ps[p][:, INTER:],
                                               ALU.mult, ALU.mult).then_inc(hid_ready, 1)

            def copy_h(w, p):
                dve.wait_ge(ht_done, w + 1)
                if not (isinstance(w, int) and w < 2):
                    dve.wait_ge(dn_done, w - 1)
                nc.vector.tensor_copy(hid_tr[p], ht_ps[p]).then_inc(htr_ready, 1)

            def hidden_shared(s):
                g, c = divmod(s, len(CHUNKS))
                rows_c = CHUNKS[c][1]
                dve.wait_ge(s_silu, s + 1)
                if g >= 2:
                    dve.wait_ge(s_down, GT * (g - 1))
                nc.vector.tensor_tensor(hid_s[g % 2][0:rows_c, c, :], act_s[s % 2][0:rows_c, :],
                                        bank[2 * (s % 2) + 1][0:rows_c, :], ALU.mult).then_inc(s_hid, 1)

            def add_z(u):
                dve.wait_ge(s_down, u + 1)
                nc.vector.tensor_tensor(resid[:, u, :], dn_ps[u % 2], resid[:, u, :], ALU.add).then_inc(z_added, 1)

            def take(t, b, before):
                if tail_tile(t):
                    src = rows[:, b, :]
                    dve.wait_ge(tail_in[b], 16)
                else:
                    src = xg[b]
                    dve.wait_ge(rows_in[b], before * 16 + 16)
                if not (isinstance(t, int) and t < DEPTH):
                    dve.wait_ge(hid_ready, t + (1 - DEPTH))
                    dve.wait_ge(y_sent[b], before * 16)
                e = dve.value_load(tile_e[0:1, bass.ds(t, 1)], min_val=0, max_val=E - 1)
                nc.vector.tensor_copy(gate_c[b][:, 0:1], src[:, bass.ds(e + L, 1)]).then_inc(gate_ready, 1)
                nc.vector.tensor_copy(dest_i[b][:, 0:1], src[:, bass.ds(e + (L + E), 1)]).then_inc(dest_ready, 1)

            add_x(UNITS - 1, 1)
            stats2(UNITS - 1, 1)
            hidden_shared(0)
            shift2(UNITS - 1, 1)
            hidden_shared(1)
            hidden_shared(2)
            less_max(1)
            hidden_shared(3)
            add_z(0)
            add_z(1)
            scores(1)
            groups(1)
            keep_groups(1)
            choose(1)
            choices(1)
            hidden_shared(4)
            marks(1)
            places(1)
            hidden_shared(5)
            dve.wait_ge(counted, 1)
            slot_of_expert(1)
            slots(1)
            rows_per_expert()
            add_z(2)
            add_z(3)
            hidden_shared(6)
            add_z(4)
            add_z(5)
            add_z(6)
            add_z(7)
            hidden_shared(7)
            tiles_per_expert()
            running_tiles()
            tile_owner()
            hidden_shared(8)
            count_owner()
            hidden_shared(9)
            add_z(8)
            add_z(9)
            tiles_before()
            count_before()
            hidden_shared(10)
            add_z(10)
            add_z(11)
            first_rows()
            last_send()
            tile_experts()
            hidden_shared(11)
            add_z(12)
            add_z(13)
            add_z(14)
            add_z(15)

            def routed_step(t, b, before):
                take(t, b, before)
                if not (isinstance(t, int) and t == 0):
                    copy_h(t - 1, 1 - b % 2)
                hidden(t, b % 2, b)

            routed(dve, routed_step)
            copy_h(TILES - 1, 1)

            for u in range(UNITS):
                b = u % DEPTH
                dve.wait_ge(fin_in[u % FIN], 16 * (u // FIN + 1))
                nc.vector.tensor_tensor(fin_a[b], fin[u % FIN][:, 0, :], fin[u % FIN][:, 1, :], ALU.add).then_inc(fc, 1)
                dve.wait_ge(fc, u + 1)
                nc.vector.tensor_tensor(fin_a[b], fin_a[b], fin[u % FIN][:, 2, :], ALU.add).then_inc(fa, 1)
                dve.wait_ge(fa, u + 1)
                dve.wait_ge(fb, u + 1)
                if u >= DEPTH:
                    dve.wait_ge(out_sent[b], 16 * (u // DEPTH))
                nc.vector.tensor_tensor(fin_o[b], fin_a[b], fin_b[b], ALU.add).then_inc(fo, 1)

        @block.tensor
        def _(pe):
            def transpose_v(u, q):
                pe.wait_ge(v_ready, u + 1)
                if not (isinstance(u, int) and u < 1):
                    pe.wait_ge(vt_ready, u)
                for blk in range(LB):
                    last = nc.tensor.transpose(tr_ps[:, blk, :], v[:, q, blk * P:(blk + 1) * P], ident[:])
                last.then_inc(vt_ps, 1)

            def convolve(u, q, g):
                pe.wait_ge(toep_in[2 * q + g % 2], 16)
                if g == 0:
                    pe.wait_ge(kv0_ready, u + 1)
                    pe.wait_ge(kv1_ready, u + 1)
                if not (isinstance(u, int) and u < 1):
                    pe.wait_ge(prod_ready, u * 4 + (g - 3))
                for s in range(2):
                    h = HEADS[g] + 2 * s
                    nc.tensor.matmul(y_ps[g][:, s, :], kv[:, q, 0, h * P:(h + 1) * P], toep[:, q * HH + h, :],
                                     start=True, stop=False)
                    last = nc.tensor.matmul(y_ps[g][:, s, P:], kv[:, q, 1, h * P:(h + 1) * P],
                                            toep[:, q * HH + h, 0:P], start=False, stop=True)
                last.then_inc(conv_done, 1)

            def sums(u, par):
                pe.wait_ge(sums_ready, 2)
                pe.wait_ge(prod_ready, u * 4 + 2 + 2 * par)
                if par == 0 and not (isinstance(u, int) and u < 1):
                    pe.wait_ge(xa_ready, u)
                for c in range(4):
                    last = nc.tensor.matmul(bank[4][32 * c:32 * c + 32, 0:L], sum_i[:, par, :],
                                            prod[:, 2 * par + c // 2, c % 2, :], start=par == 0, stop=par == 1)
                last.then_inc(sum_done if par else even_done, 1)

            def skip_sum(u, q):
                pe.wait_ge(skipw_ready, 2)
                pe.wait_ge(vc_ready, u + 1)
                if not (isinstance(u, int) and u < 1):
                    pe.wait_ge(skip_ready, u)
                nc.tensor.matmul(g_ps, skip_w[:, q, :], vc[:, q, :], start=True, stop=True).then_inc(g_done, 1)

            def transpose_xn(u, q):
                pe.wait_ge(xn_ready, u + 1)
                if not (isinstance(u, int) and u < 1):
                    pe.wait_ge(logits_ready, u)
                for blk in range(LB):
                    last = nc.tensor.transpose(xn_ps[:, blk, :], xn[:, q, blk * P:(blk + 1) * P], ident[:])
                last.then_inc(xt_done, 1)

            def router(u, q):
                pe.wait_ge(wg_in, 16)
                pe.wait_ge(xnt_ready, u + 1)
                pe.wait_ge(xnt_all, u + 1)
                for blk in range(LB):
                    last = nc.tensor.matmul(logit_ps, xn_tr[:, q, blk, :], wg[:, blk, :],
                                            start=blk == 0, stop=blk == LB - 1)
                last.then_inc(logits_done, 1)

            def ranks(b):
                lo, hi = b * TB, (b + 1) * TB
                pe.wait_ge(sel_ready, b + 1)
                if b == 0:
                    pe.wait_ge(skip_ready, ROUTE0 + 3)
                else:
                    pe.wait_ge(skip_ready, UNITS)
                nc.tensor.matmul(rank_ps[b], before[:], sel_bf[:, lo:hi, :], start=True, stop=False)
                for t in range(hi - 1):
                    to = max(t + 1, lo)
                    last = nc.tensor.matmul(rank_ps[b][:, to - lo:, :], ones[:],
                                            sel_bf[:, t:t + 1, :].to_broadcast([P, hi - to, E]),
                                            start=False, stop=t == hi - 2)
                last.then_inc(rank_done, 1)

            def step(u, q, landed, first, last):
                second = not (isinstance(u, int) and u < 2)
                convolve(u, q, 0)
                if not first:
                    sums(u - 1, 1)
                convolve(u, q, 1)
                if isinstance(u, int) and u == ROUTE0 + 3:
                    ranks(0)
                skip_sum(u, q)
                if not last:
                    transpose_v(u + 1, 1 - q)
                if second:
                    transpose_xn(u - 2, q)
                convolve(u, q, 2)
                sums(u, 0)
                if second:
                    router(u - 2, q)
                convolve(u, q, 3)

            pe.wait_ge(const, C_IDENT)
            transpose_v(0, 0)

            units(pe, step, lambda u: None)

            expert_of = [pe.alloc_register(f"expert_of{b}") for b in range(DEPTH)]

            def up(t, p, b):
                pe.reg_load(expert_of[b], tile_e[0:1, bass.ds(t, 1)])
                e = pe.snap(expert_of[b], min_val=0, max_val=E - 1)
                if not (isinstance(t, int) and t < 2):
                    pe.wait_ge(hid_ready, t - 1)
                pe.wait_ge(xtr_ready, t + 1)
                for blk in range(LB):
                    last = nc.tensor.matmul(up_ps[p], x_tr[p][:, blk, :],
                                            w13[:, bass.ds(e, 1), blk, :].rearrange("p a n -> p (a n)"),
                                            start=blk == 0, stop=blk == LB - 1)
                last.then_inc(up_done, 1)

            def turn_h(w, p):
                pe.wait_ge(hid_ready, w + 1)
                if not (isinstance(w, int) and w < 2):
                    pe.wait_ge(htr_ready, w - 1)
                for c in range(2):
                    last = nc.tensor.transpose(ht_ps[p][:, c, :], hid[p][:, c * HI:(c + 1) * HI], ident[:])
                last.then_inc(ht_done, 1)

            def turn_x(t, p, b, before):
                if tail_tile(t):
                    src = rows[:, b, :]
                    pe.wait_ge(tail_in[b], 16)
                else:
                    src = xg[b]
                    pe.wait_ge(rows_in[b], before * 16 + 16)
                if not (isinstance(t, int) and t < 2):
                    pe.wait_ge(xtr_ready, t - 1)
                for blk in range(LB):
                    last = nc.tensor.transpose(xt_ps[p][:, blk, :], src[:, blk * P:(blk + 1) * P], ident[:])
                last.then_inc(xtr_ps, 1)

            def up_shared(s):
                g, c = divmod(s, len(CHUNKS))
                c0, rows_c = CHUNKS[c]
                if s >= 2:
                    pe.wait_ge(s_hid, s - 1)
                pe.wait_ge(xnt_all, GT * (g + 1))
                for w in range(2):
                    for blk in range(LB):
                        last = nc.tensor.matmul(
                            bank[2 * (s % 2) + w][0:rows_c, :].rearrange("p (u n) -> p u n", u=GT),
                            ws13[:, blk, w, c0:c0 + rows_c], xn_tr_all[:, GT * g:GT * (g + 1), blk, :],
                            start=blk == 0, stop=blk == LB - 1)
                last.then_inc(s_up, 1)

            def down_shared(u):
                g, i = divmod(u, GT)
                pe.wait_ge(s_hid, len(CHUNKS) * (g + 1))
                if u >= 2:
                    pe.wait_ge(z_added, u - 1)
                for c, (_, rows_c) in enumerate(CHUNKS):
                    last = nc.tensor.matmul(dn_ps[u % 2], hid_s[g % 2][0:rows_c, c, i * P:(i + 1) * P],
                                            ws2[0:rows_c, c, :], start=c == 0, stop=c == len(CHUNKS) - 1)
                last.then_inc(s_down, 1)

            def down(t, p, b):
                e = pe.snap(expert_of[b], min_val=0, max_val=E - 1)
                if not (isinstance(t, int) and t < 2):
                    pe.wait_ge(y_ready, t - 1)
                pe.wait_ge(htr_ready, t + 1)
                for c in range(2):
                    last = nc.tensor.matmul(dn_ps[p], hid_tr[p][:, c, :],
                                            w2[:, bass.ds(e, 1), c, :].rearrange("p a n -> p (a n)"),
                                            start=c == 0, stop=c == 1)
                last.then_inc(dn_done, 1)

            sums(UNITS - 1, 1)
            pe.wait_ge(wsh_in, 48)
            pe.wait_ge(prod_ready, 4 * UNITS)
            up_shared(0)
            transpose_xn(UNITS - 2, 0)
            up_shared(1)
            router(UNITS - 2, 0)
            transpose_xn(UNITS - 1, 1)
            up_shared(2)
            router(UNITS - 1, 1)
            up_shared(3)
            pe.wait_ge(xa_ready, UNITS)
            pe.wait_ge(skip_ready, UNITS)
            for s in range(4, GROUPS * len(CHUNKS) + 1):
                g, c = divmod(s - 1, len(CHUNKS))
                if c < 2:
                    down_shared(GT * (g - 1) + 2 * c)
                    down_shared(GT * (g - 1) + 2 * c + 1)
                if s == 6:
                    ranks(1)
                    pe.wait_ge(vt_ready, UNITS)
                    nc.tensor.matmul(count_ps, ones[:], sel_bf[:], start=True, stop=True).then_inc(counted, 1)
                if s < GROUPS * len(CHUNKS):
                    up_shared(s)
            for u in range(UNITS - GT, UNITS):
                down_shared(u)
            pe.wait_ge(w_in, 32 * E)
            pe.wait_ge(map_ready, 1)
            pe.wait_ge(logits_ready, UNITS)
            for _ in range(KEEP_WARM):
                nc.tensor.transpose(xt_ps[1][:, 0, :], ident[:], ident[:])
            turn_x(0, 0, 0, 0)
            pe.wait_ge(z_added, UNITS)

            def routed_step(t, b, before):
                p = b % 2
                up(t, p, b)
                if not (isinstance(t, int) and t == 0):
                    turn_h(t - 1, 1 - p)
                if not (isinstance(t, int) and t == TILES - 1):
                    turn_x(t + 1, 1 - p, (b + 1) % DEPTH, before + 1 if b == DEPTH - 1 else before)
                if not (isinstance(t, int) and t < 2):
                    down(t - 2, p, (b - 2) % DEPTH)

            routed(pe, routed_step)
            turn_h(TILES - 1, 1)
            down(TILES - 2, 0, DEPTH - 2)
            down(TILES - 1, 1, DEPTH - 1)


def kernel(x, fside_S2_0, ctx_2048, L0_xattn_k, L0_ffn_Wg, L0_ffn_W1, L0_ffn_W3, L0_ffn_W2, L0_ffn_Ws1, L0_ffn_Ws3,
           L0_ffn_Ws2):
    import concourse.bacc as bacc
    from concourse.bass_utils import run_bass_kernel_spmd

    def tiles(a):
        a = np.asarray(a).reshape(B // 2, 2, 2, HH, C, L).transpose(0, 2, 3, 1, 4, 5)
        return a.reshape(UNITS, P, L)

    ctx_u = tiles(ctx_2048)
    ctx_g = np.asarray(ctx_2048).reshape(B // 2, 2, 2, HH, C, L).transpose(0, 2, 1, 4, 3, 5)
    up_w = np.concatenate([np.asarray(L0_ffn_W1), np.asarray(L0_ffn_W3)], axis=1)
    up_s = np.stack([np.asarray(L0_ffn_Ws1), np.asarray(L0_ffn_Ws3)])
    arrays = {
        "x_in": tiles(x),
        "ctx_in": ctx_u,
        "ctxt_in": ctx_u.reshape(UNITS, P, LB, P)[:, :, :, ::-1].transpose(0, 3, 2, 1).reshape(UNITS, P, L),
        "ctxr_in": ctx_g.reshape(UNITS, 2 * C, HH * L),
        "k_in": L0_xattn_k,
        "bias_in": np.repeat(np.asarray(fside_S2_0).reshape(2, HH, 1, C), 2, axis=2).reshape(2, P).T,
        "wg_in": np.asarray(L0_ffn_Wg).T.reshape(LB, P, E).transpose(1, 0, 2),
        "w13_in": up_w.reshape(E, 2 * INTER, LB, P).transpose(3, 0, 2, 1),
        "w2_in": np.asarray(L0_ffn_W2).reshape(E, L, 2, HI).transpose(3, 0, 2, 1),
        "ws13_in": up_s.reshape(2, SW, LB, P).transpose(3, 2, 0, 1),
        "ws2_in": np.asarray(L0_ffn_Ws2).T,
    }
    arrays = {n: np.ascontiguousarray(a) for n, a in arrays.items()}
    nc = bacc.Bacc("TRN2", target_bir_lowering=False, num_devices=1, dynamic_dma_scratch_size=8192)
    ins = [nc.dram_tensor(n, a.shape, mybir.dt.from_np(a.dtype), kind="ExternalInput").ap() for n, a in arrays.items()]
    out = nc.dram_tensor("out", (UNITS, P, L), F32, kind="ExternalOutput").ap()
    build(nc, *ins, out)
    got = run_bass_kernel_spmd(nc, [arrays], core_ids=[0]).results[0]["out"]
    got = np.asarray(got).reshape(B // 2, 2, HH, 2, C, L).transpose(0, 3, 1, 2, 4, 5)
    return np.ascontiguousarray(got.reshape(B, D, L))
```
